# Optimizing a Trainium2 kernel written in Bass

```python
import numpy as np
import jax
import jax.numpy as jnp

def _softmax(x, axis=-1):
    return jax.nn.softmax(x, axis=axis)

def _gelu(x):
    return jax.nn.gelu(x, approximate=True)

def _silu(x):
    return jax.nn.silu(x)

def _sigmoid(x):
    return jax.nn.sigmoid(x)

def _layernorm(x, axis=-1, eps=1e-05):
    m = jnp.mean(x, axis=axis, keepdims=True)
    v = jnp.var(x, axis=axis, keepdims=True)
    return (x - m) / jnp.sqrt(v + eps)

def _scatter_add(tgt, idx, src, axis=0):
    return tgt.at[idx].add(src)

def _segment_sum(src, seg, n):
    return jax.ops.segment_sum(src, seg, n)
kernel_name = 'mk_dlrm_tower_d1_rec_r8_d5b4e5'

def setup_inputs(seed: int=0):
    np.random.seed(seed)
    _w = jnp.asarray

    def _rec_inputs():
        import jax
        import jax.numpy as jnp
        _tk = jax.random.key(seed)
        dense_ctx = jax.random.normal(jax.random.fold_in(_tk, 190), (2048, 16), jnp.float32)
        ids = jnp.stack([jax.random.randint(jax.random.fold_in(_tk, 200 + f), (2048,), 0, v, jnp.int32) for f, v in enumerate([1000, 1000, 1000, 125000, 1000, 125000, 1000, 12500, 1000, 125000, 12500, 12500, 125000, 1000, 12500, 125000, 125000, 12500, 1250, 125000, 1250, 12500, 12500, 1000, 1250, 1250, 1000, 1250, 1000, 1000, 1250, 1000])], axis=1)
        tbl_0 = 0.05 * jax.random.normal(jax.random.fold_in(_tk, 500 + 0), (1000, 32), jnp.float32)
        tbl_1 = 0.05 * jax.random.normal(jax.random.fold_in(_tk, 500 + 1), (1000, 32), jnp.float32)
        tbl_2 = 0.05 * jax.random.normal(jax.random.fold_in(_tk, 500 + 2), (1000, 32), jnp.float32)
        tbl_3 = 0.05 * jax.random.normal(jax.random.fold_in(_tk, 500 + 3), (125000, 32), jnp.float32)
        tbl_4 = 0.05 * jax.random.normal(jax.random.fold_in(_tk, 500 + 4), (1000, 32), jnp.float32)
        tbl_5 = 0.05 * jax.random.normal(jax.random.fold_in(_tk, 500 + 5), (125000, 32), jnp.float32)
        tbl_6 = 0.05 * jax.random.normal(jax.random.fold_in(_tk, 500 + 6), (1000, 32), jnp.float32)
        tbl_7 = 0.05 * jax.random.normal(jax.random.fold_in(_tk, 500 + 7), (12500, 32), jnp.float32)
        tbl_8 = 0.05 * jax.random.normal(jax.random.fold_in(_tk, 500 + 8), (1000, 32), jnp.float32)
        tbl_9 = 0.05 * jax.random.normal(jax.random.fold_in(_tk, 500 + 9), (125000, 32), jnp.float32)
        tbl_10 = 0.05 * jax.random.normal(jax.random.fold_in(_tk, 500 + 10), (12500, 32), jnp.float32)
        tbl_11 = 0.05 * jax.random.normal(jax.random.fold_in(_tk, 500 + 11), (12500, 32), jnp.float32)
        tbl_12 = 0.05 * jax.random.normal(jax.random.fold_in(_tk, 500 + 12), (125000, 32), jnp.float32)
        tbl_13 = 0.05 * jax.random.normal(jax.random.fold_in(_tk, 500 + 13), (1000, 32), jnp.float32)
        tbl_14 = 0.05 * jax.random.normal(jax.random.fold_in(_tk, 500 + 14), (12500, 32), jnp.float32)
        tbl_15 = 0.05 * jax.random.normal(jax.random.fold_in(_tk, 500 + 15), (125000, 32), jnp.float32)
        tbl_16 = 0.05 * jax.random.normal(jax.random.fold_in(_tk, 500 + 16), (125000, 32), jnp.float32)
        tbl_17 = 0.05 * jax.random.normal(jax.random.fold_in(_tk, 500 + 17), (12500, 32), jnp.float32)
        tbl_18 = 0.05 * jax.random.normal(jax.random.fold_in(_tk, 500 + 18), (1250, 32), jnp.float32)
        tbl_19 = 0.05 * jax.random.normal(jax.random.fold_in(_tk, 500 + 19), (125000, 32), jnp.float32)
        tbl_20 = 0.05 * jax.random.normal(jax.random.fold_in(_tk, 500 + 20), (1250, 32), jnp.float32)
        tbl_21 = 0.05 * jax.random.normal(jax.random.fold_in(_tk, 500 + 21), (12500, 32), jnp.float32)
        tbl_22 = 0.05 * jax.random.normal(jax.random.fold_in(_tk, 500 + 22), (12500, 32), jnp.float32)
        tbl_23 = 0.05 * jax.random.normal(jax.random.fold_in(_tk, 500 + 23), (1000, 32), jnp.float32)
        tbl_24 = 0.05 * jax.random.normal(jax.random.fold_in(_tk, 500 + 24), (1250, 32), jnp.float32)
        tbl_25 = 0.05 * jax.random.normal(jax.random.fold_in(_tk, 500 + 25), (1250, 32), jnp.float32)
        tbl_26 = 0.05 * jax.random.normal(jax.random.fold_in(_tk, 500 + 26), (1000, 32), jnp.float32)
        tbl_27 = 0.05 * jax.random.normal(jax.random.fold_in(_tk, 500 + 27), (1250, 32), jnp.float32)
        tbl_28 = 0.05 * jax.random.normal(jax.random.fold_in(_tk, 500 + 28), (1000, 32), jnp.float32)
        tbl_29 = 0.05 * jax.random.normal(jax.random.fold_in(_tk, 500 + 29), (1000, 32), jnp.float32)
        tbl_30 = 0.05 * jax.random.normal(jax.random.fold_in(_tk, 500 + 30), (1250, 32), jnp.float32)
        tbl_31 = 0.05 * jax.random.normal(jax.random.fold_in(_tk, 500 + 31), (1000, 32), jnp.float32)
        _rk = jax.random.fold_in(_tk, 7)
        W_top1 = 0.0830455 * jax.random.normal(jax.random.fold_in(_tk, 801), (145, 512), jnp.float32)
        W_top2 = 0.0441942 * jax.random.normal(jax.random.fold_in(_tk, 802), (512, 256), jnp.float32)
        W_top3 = 0.0625 * jax.random.normal(jax.random.fold_in(_tk, 803), (256, 1), jnp.float32)
        b_top1 = jnp.zeros((512,), jnp.float32)
        b_top2 = jnp.zeros((256,), jnp.float32)
        return (dense_ctx, ids, tbl_0, tbl_1, tbl_2, tbl_3, tbl_4, tbl_5, tbl_6, tbl_7, tbl_8, tbl_9, tbl_10, tbl_11, tbl_12, tbl_13, tbl_14, tbl_15, tbl_16, tbl_17, tbl_18, tbl_19, tbl_20, tbl_21, tbl_22, tbl_23, tbl_24, tbl_25, tbl_26, tbl_27, tbl_28, tbl_29, tbl_30, tbl_31, W_top1, b_top1, W_top2, b_top2, W_top3)
    dense_ctx, ids, tbl_0, tbl_1, tbl_2, tbl_3, tbl_4, tbl_5, tbl_6, tbl_7, tbl_8, tbl_9, tbl_10, tbl_11, tbl_12, tbl_13, tbl_14, tbl_15, tbl_16, tbl_17, tbl_18, tbl_19, tbl_20, tbl_21, tbl_22, tbl_23, tbl_24, tbl_25, tbl_26, tbl_27, tbl_28, tbl_29, tbl_30, tbl_31, W_top1, b_top1, W_top2, b_top2, W_top3 = _rec_inputs()

    def _L0_rec_setup():
        import jax, jax.numpy as jnp
        import numpy as np

        def _cin(x, Ws, bs):
            B, F, D = x.shape
            h = x
            directs = []
            n_layers = len(Ws)
            for i, (W, b) in enumerate(zip(Ws, bs)):
                O = W.shape[0]
                H = h.shape[1]
                z = jnp.einsum('bhd,bmd,ohm->bod', h, x, W.reshape(O, H, F))
                z = jax.nn.relu(z + b[None, :, None])
                if i < n_layers - 1:
                    half = O // 2
                    h, direct = (z[:, :half, :], z[:, half:, :])
                else:
                    direct = z
                directs.append(direct)
            out = jnp.concatenate(directs, axis=1)
            return jnp.sum(out, axis=-1)
        key = jax.random.key(seed)
        ks = jax.random.split(key, 4)
        B, F, D = (256, 32, 32)
        x = jax.random.normal(ks[0], (B, F, D), dtype=jnp.float32)
        W0 = jax.random.normal(ks[1], (128, 32 * F), dtype=jnp.float32) * 0.05
        W1 = jax.random.normal(ks[2], (128, 64 * F), dtype=jnp.float32) * 0.05
        W2 = jax.random.normal(ks[3], (1, 64 * F), dtype=jnp.float32) * 0.05
        return {'x': x, 'W0': W0, 'b0': jnp.zeros((128,), jnp.float32), 'W1': W1, 'b1': jnp.zeros((128,), jnp.float32), 'W2': W2, 'b2': jnp.zeros((1,), jnp.float32)}
    _L0_rec_all = _L0_rec_setup()
    _L0_rec_in = {k: v for k, v in _L0_rec_all.items() if k in ('W0', 'b0', 'W1', 'b1', 'W2', 'b2')}
    del _L0_rec_all
    return {'dense_ctx': dense_ctx, 'ids': ids, 'tbl_0': tbl_0, 'tbl_1': tbl_1, 'tbl_2': tbl_2, 'tbl_3': tbl_3, 'tbl_4': tbl_4, 'tbl_5': tbl_5, 'tbl_6': tbl_6, 'tbl_7': tbl_7, 'tbl_8': tbl_8, 'tbl_9': tbl_9, 'tbl_10': tbl_10, 'tbl_11': tbl_11, 'tbl_12': tbl_12, 'tbl_13': tbl_13, 'tbl_14': tbl_14, 'tbl_15': tbl_15, 'tbl_16': tbl_16, 'tbl_17': tbl_17, 'tbl_18': tbl_18, 'tbl_19': tbl_19, 'tbl_20': tbl_20, 'tbl_21': tbl_21, 'tbl_22': tbl_22, 'tbl_23': tbl_23, 'tbl_24': tbl_24, 'tbl_25': tbl_25, 'tbl_26': tbl_26, 'tbl_27': tbl_27, 'tbl_28': tbl_28, 'tbl_29': tbl_29, 'tbl_30': tbl_30, 'tbl_31': tbl_31, 'W_top1': W_top1, 'b_top1': b_top1, 'W_top2': W_top2, 'b_top2': b_top2, 'W_top3': W_top3, 'L0_rec_W0': _L0_rec_in['W0'], 'L0_rec_b0': _L0_rec_in['b0'], 'L0_rec_W1': _L0_rec_in['W1'], 'L0_rec_b1': _L0_rec_in['b1'], 'L0_rec_W2': _L0_rec_in['W2'], 'L0_rec_b2': _L0_rec_in['b2']}

def reference(dense_ctx, ids, tbl_0, tbl_1, tbl_2, tbl_3, tbl_4, tbl_5, tbl_6, tbl_7, tbl_8, tbl_9, tbl_10, tbl_11, tbl_12, tbl_13, tbl_14, tbl_15, tbl_16, tbl_17, tbl_18, tbl_19, tbl_20, tbl_21, tbl_22, tbl_23, tbl_24, tbl_25, tbl_26, tbl_27, tbl_28, tbl_29, tbl_30, tbl_31, W_top1, b_top1, W_top2, b_top2, W_top3, L0_rec_W0, L0_rec_b0, L0_rec_W1, L0_rec_b1, L0_rec_W2, L0_rec_b2):
    import jax
    import jax.numpy as jnp

    def _L0_rec_ref(x, W0, b0, W1, b1, W2, b2):
        import jax, jax.numpy as jnp
        import numpy as np

        def _cin(x, Ws, bs):
            B, F, D = x.shape
            h = x
            directs = []
            n_layers = len(Ws)
            for i, (W, b) in enumerate(zip(Ws, bs)):
                O = W.shape[0]
                H = h.shape[1]
                z = jnp.einsum('bhd,bmd,ohm->bod', h, x, W.reshape(O, H, F))
                z = jax.nn.relu(z + b[None, :, None])
                if i < n_layers - 1:
                    half = O // 2
                    h, direct = (z[:, :half, :], z[:, half:, :])
                else:
                    direct = z
                directs.append(direct)
            out = jnp.concatenate(directs, axis=1)
            return jnp.sum(out, axis=-1)
        return _cin(x, (W0, W1, W2), (b0, b1, b2))
    e = jnp.stack([tbl_0[ids[:, 0]], tbl_1[ids[:, 1]], tbl_2[ids[:, 2]], tbl_3[ids[:, 3]], tbl_4[ids[:, 4]], tbl_5[ids[:, 5]], tbl_6[ids[:, 6]], tbl_7[ids[:, 7]], tbl_8[ids[:, 8]], tbl_9[ids[:, 9]], tbl_10[ids[:, 10]], tbl_11[ids[:, 11]], tbl_12[ids[:, 12]], tbl_13[ids[:, 13]], tbl_14[ids[:, 14]], tbl_15[ids[:, 15]], tbl_16[ids[:, 16]], tbl_17[ids[:, 17]], tbl_18[ids[:, 18]], tbl_19[ids[:, 19]], tbl_20[ids[:, 20]], tbl_21[ids[:, 21]], tbl_22[ids[:, 22]], tbl_23[ids[:, 23]], tbl_24[ids[:, 24]], tbl_25[ids[:, 25]], tbl_26[ids[:, 26]], tbl_27[ids[:, 27]], tbl_28[ids[:, 28]], tbl_29[ids[:, 29]], tbl_30[ids[:, 30]], tbl_31[ids[:, 31]]], axis=1)
    z = _L0_rec_ref(e, L0_rec_W0, L0_rec_b0, L0_rec_W1, L0_rec_b1, L0_rec_W2, L0_rec_b2)
    z = z.reshape(z.shape[0], -1)
    h = jnp.concatenate([z, dense_ctx], axis=1)
    h = jnp.maximum(h @ W_top1 + b_top1, 0.0)
    h = jnp.maximum(h @ W_top2 + b_top2, 0.0)
    y = h @ W_top3
    return y

_drawn_inputs = setup_inputs


def setup_inputs(seed=0):
    import zlib

    import numpy as np

    out = dict(_drawn_inputs(seed))
    spreads = {'b_top1': (0.0, 2.0),
     'b_top2': (0.0, 0.458),
     'L0_rec_b0': (0.0, 0.1),
     'L0_rec_b1': (0.0, 0.1)}
    factors = {'tbl_0': 8.0,
     'tbl_1': 8.0,
     'tbl_2': 8.0,
     'tbl_3': 8.0,
     'tbl_4': 8.0,
     'tbl_5': 8.0,
     'tbl_6': 8.0,
     'tbl_7': 8.0,
     'tbl_8': 8.0,
     'tbl_9': 8.0,
     'tbl_10': 8.0,
     'tbl_11': 8.0,
     'tbl_12': 8.0,
     'tbl_13': 8.0,
     'tbl_14': 8.0,
     'tbl_15': 8.0,
     'tbl_16': 8.0,
     'tbl_17': 8.0,
     'tbl_18': 8.0,
     'tbl_19': 8.0,
     'tbl_20': 8.0,
     'tbl_21': 8.0,
     'tbl_22': 8.0,
     'tbl_23': 8.0,
     'tbl_24': 8.0,
     'tbl_25': 8.0,
     'tbl_26': 8.0,
     'tbl_27': 8.0,
     'tbl_28': 8.0,
     'tbl_29': 8.0,
     'tbl_30': 8.0,
     'tbl_31': 8.0,
     'L0_rec_W0': 8.0,
     'L0_rec_W1': 3.571,
     'L0_rec_W2': 8.0,
     'dense_ctx': 3.643}
    for name, (base, spread) in spreads.items():
        noise = np.random.default_rng([zlib.crc32(name.encode()), seed]).standard_normal(out[name].shape)
        drawn = base * np.exp(spread * noise) if base else spread * noise
        out[name] = jnp.asarray(drawn.astype(out[name].dtype))
    for name, factor in factors.items():
        out[name] = (out[name] * factor).astype(out[name].dtype)
    return out
```

```python
import concourse.bass as bass
from concourse import mybir
from contextlib import ExitStack

F32 = mybir.dt.float32
F32R = mybir.dt.float32r
I32 = mybir.dt.int32
ALU = mybir.AluOpType
ACT = mybir.ActivationFunctionType
AX = mybir.AxisListType

B, F, D = 2048, 32, 32
O = 128
H = O // 2
DENSE, HID1, HID2 = 16, 512, 256
G = B // 128
CH = 8
T = 512
SB = T // D
NQ = G * CH
L0_TILES = 4
L1_TILES = 16
N_SEL = L0_TILES + 1 + L1_TILES
LAG = 3
RING = LAG + 1
PIECE_DMAS = 6

L0_SLOTS = [("L0", 0), ("L0", 1), ("L0x", 0)]
STREAM = [("L1", 0), ("L1", 1), ("L1", 2), ("L1", 3)] + L0_SLOTS + [("L1", 4), ("L1", 5), ("L1", 6), ("L1", 7)]
NS = len(STREAM)
L0X_AT = STREAM.index(("L0x", 0))
SUB = {("L1", 0): "g", ("L1", 1): "v", ("L1", 2): "g", ("L1", 3): "v", ("L0", 0): "g", ("L0", 1): "v",
       ("L0x", 0): "v", ("L1", 4): "g", ("L1", 5): "v", ("L1", 6): "g", ("L1", 7): "v"}
AT_Z1 = 3
AT_Z0 = 9
AT_H1LO = 5
AT_DIRECT = 6
AT_V = 6
AT_Q = 8
AT_X = 7
LOAD_C = 5


class Slot:

    def __init__(self, g, c, s, kind, prologue=False):
        self.kind, self.tile = kind
        self.sub = SUB[kind]
        self.first = 0 if prologue else len(L0_SLOTS)
        q = CH * g + c
        self.ring = (s if prologue else len(L0_SLOTS) + NS * c + s) % RING
        self.bank = (s if prologue else len(L0_SLOTS) + NS * c + s) % 2
        self.done = s + 1 if prologue else q * NS + (len(L0_SLOTS) + s + 1)
        before = L0_SLOTS[:s + 1] if prologue else L0_SLOTS + STREAM[:s + 1]

        def count(what):
            n = sum(SUB[k] in what for k in before)
            return n if prologue else q * sum(SUB[k] in what for k in STREAM) + n

        self.hi, self.lo_v, self.lo_g = count(("v", "g")), count(("v",)), count(("g",))
        if self.kind == "L1":
            self.piece, self.q = c, q
        elif prologue:
            self.piece, self.q, self.group = 0, 0, 0
        else:
            self.piece, self.q = (c + 1) % CH, q + 1
            self.group = g + (c + 1) // CH


def slots_of(g, c, last=False):
    stream = [k for k in STREAM if k[0] == "L1"] if last else STREAM
    out = []
    for s, kind in enumerate(stream):
        x = Slot(g, c, s, kind)
        if last:
            q = CH * g + c
            full = L0_SLOTS + STREAM * q + stream[:s + 1]
            x.hi = sum(SUB[k] != "" for k in full)
            x.lo_v = sum(SUB[k] == "v" for k in full)
            x.lo_g = sum(SUB[k] == "g" for k in full)
        out.append(x)
    return out


def back(g, c, s, k, slots):
    if s >= k:
        return slots[s - k]
    if c == 0 and isinstance(g, int) and g == 0:
        return None
    return slots_of(g - 1 if c == 0 else g, (c - 1) % CH)[s - k]


def build(nc, tables, dense_ctx, ids, W_top1, b_top1, W_top2, b_top2, W_top3, W0, b0, W1, b1, W2, b2,
          sel_c, ident_c, ones_c, out):
    ctx = ExitStack()
    with ctx:
        def sb(name, shape, dt=F32):
            return ctx.enter_context(nc.sbuf_tensor(name, shape, dt))

        def ps(name, shape):
            return ctx.enter_context(nc.psum_tensor(name, shape, F32))

        def sem(name):
            return ctx.enter_context(nc.semaphore(name))

        idx = sb("idx", [128, F], I32)
        rows = sb("rows", [128, F * D])
        X = sb("X", [128, 2 * T])
        Xhi = sb("Xhi", [128, 2 * T], F32R)
        Xlo = sb("Xlo", [128, 2 * T], F32R)
        S = sb("S", [128, CH, T], F32R)
        xrep = sb("xrep", [128, CH, T])
        XQ = sb("XQ", [128, 2, T])
        P = sb("P", [128, RING, 2, T])
        Phi = sb("Phi", [128, RING, 2, T], F32R)
        Plo = sb("Plo", [128, RING, 2, T], F32R)
        hdup = sb("hdup", [128, 2, T])
        direct = sb("direct", [128, 2, T])
        h1f = sb("h1f", [H, T])
        h1 = sb("h1", [128, T], F32R)
        Qp = sb("Qp", [128, T])
        Qt = sb("Qt", [128, T])
        z2s = sb("z2s", [128, G * 2, SB])
        z2r = sb("z2r", [128, G * 2 * SB])
        feat = sb("feat", [128, 4, G * 2 * SB])
        aux = sb("aux", [36, 4, T])
        Sel = sb("Sel", [128, N_SEL, 128], F32R)
        Whi = sb("Whi", [128, N_SEL, 128], F32R)
        Wlo = sb("Wlo", [128, N_SEL, 128], F32R)
        whole = any(v == "" for v in SUB.values())
        Wf = sb("Wf", [128, N_SEL, 128]) if whole else None
        w2f = sb("w2f", [128, F])
        W2p = sb("W2p", [128, 2, 4, 128], F32R)
        ws = sb("ws", [128, 5, 128])
        ident = sb("ident", [128, 128])
        ones4 = sb("ones4", [128, 4])
        b0t, b1t, b2t = sb("b0t", [128, 1]), sb("b1t", [128, 1]), sb("b2t", [128, 1])
        bt1, bt2 = sb("bt1", [128, 4]), sb("bt2", [128, 2])
        wt1 = sb("wt1", [128, HID1])
        wta = sb("wta", [36, 4, HID1])
        wt2 = sb("wt2", [128, 4, HID2])
        wt3 = sb("wt3", [128, 2, 1])
        dense = sb("dense", [128, G, DENSE])
        y = sb("y", [1, 4, T])
        w1s = P[:, 0:2, :, :].rearrange("p r t n -> p (r t n)")
        w1p = P[:, 2:4, :, :].rearrange("p r t n -> p (r t n)")
        flat = xrep[:, :, :].rearrange("p c n -> p (c n)")
        selF = flat[:, 0:N_SEL * 128]
        w0s = flat[:, 3072:4096]
        hid1 = P[:, :, :, :].rearrange("p (e r) t n -> p e (r t) n", e=2)
        hid2 = xrep[:, 0:4, :].rearrange("p (e m) n -> p e m n", e=2)

        pB = ps("pB", [128, 2, 2, T])
        pz0 = ps("pz0", [128, T])
        pz1 = ps("pz1", [128, 2, T])
        pV = ps("pV", [128, T])

        setup_w = sem("setup_w")
        setup_c = sem("setup_c")
        idx_loaded = sem("idx_loaded")
        gathered = sem("gathered")
        zeroed = sem("zeroed")
        w1_laid = sem("w1_laid")
        ws_laid = sem("ws_laid")
        w_turned = sem("w_turned")
        w_hi = sem("w_hi")
        w_lo = sem("w_lo")
        sel_ready = sem("sel_ready")
        x_ready = sem("x_ready")
        xhi_ready = sem("xhi_ready")
        xlo_ready = sem("xlo_ready")
        piece_loaded = [sem(f"piece_loaded{c}") for c in range(CH)]
        xq_loaded = [sem(f"xq_loaded{h}") for h in range(2)]
        bcast_ready = sem("bcast_ready")
        product_ready = sem("product_ready")
        hi_ready = sem("hi_ready")
        lo_v_ready = sem("lo_v_ready")
        lo_g_ready = sem("lo_g_ready")
        main_done = sem("main_done")
        h0_ready = sem("h0_ready")
        z0_read = sem("z0_read")
        h1_ready = sem("h1_ready")
        h1lo_ready = sem("h1lo_ready")
        z1_read = sem("z1_read")
        direct_used = sem("direct_used")
        v_done = sem("v_done")
        q_done = sem("q_done")
        qt_done = sem("qt_done")
        z2_sum = sem("z2_sum")
        z2_relu = sem("z2_relu")
        z2_row = sem("z2_row")
        dense_turned = sem("dense_turned")
        aux_ready = sem("aux_ready")
        hid1_done, hid1_act = sem("hid1_done"), sem("hid1_act")
        hid2_done, hid2_act = sem("hid2_done"), sem("hid2_act")
        y_done, y_copied, stored = sem("y_done"), sem("y_copied"), sem("stored")

        ids_g = ids.rearrange("(g p) f -> g p f", p=128)
        block = ctx.enter_context(nc.Block())

        @block.sync
        def _(sp):
            def load_idx(g):
                sp.dma_start(idx[:, :], ids_g[g]).then_inc(idx_loaded, 16)

            def load_piece(c):
                part = slice(32 * (c % 4), 32 * (c % 4) + 32)
                cols = slice(T * (c // 4), T * (c // 4) + T)
                sp.dma_start(S[0:32, c, :].bitcast(F32), Xhi[part, cols].bitcast(F32)).then_inc(piece_loaded[c], 16)
                sp.dma_start(S[32:64, c, :].bitcast(F32), Xlo[part, cols].bitcast(F32)).then_inc(piece_loaded[c], 16)
                for r in range(4):
                    sp.dma_start(xrep[32 * r:32 * r + 32, c, :], X[part, cols]).then_inc(piece_loaded[c], 16)

            def load_xq(half):
                sp.dma_start(XQ[:, half, :], X[:, half * T:half * T + T]).then_inc(xq_loaded[half], 16)

            load_idx(0)
            sp.dma_start(w0s, W0).then_inc(setup_w, 16)
            sp.dma_start(ident[:, :], ident_c).then_inc(setup_w, 16)
            sp.dma_start(w1s, W1).then_inc(setup_w, 16)
            sp.dma_start(w2f[0:H, :], W2.rearrange("o (h m) -> (o h) m", m=F)).then_inc(setup_w, 16)
            sp.dma_start(w2f[H:128, :], W2.rearrange("o (h m) -> (o h) m", m=F)).then_inc(setup_w, 16)
            sp.dma_start(selF, sel_c).then_inc(setup_w, 16)
            sp.dma_start(b0t[:, :], b0.rearrange("(p o) -> p o", o=1)).then_inc(setup_w, 16)
            sp.dma_start(b1t[:, :], b1.rearrange("(p o) -> p o", o=1)).then_inc(setup_w, 16)
            sp.wait_ge(xlo_ready, 1)
            sp.wait_ge(ws_laid, 1)
            sp.wait_ge(sel_ready, 1)
            for c in range(CH):
                load_piece(c)
                if c == 3:
                    load_xq(0)
            load_xq(1)
            sp.wait_ge(zeroed, 3)
            sp.dma_start(ones4[:, :], ones_c).then_inc(setup_c, 16)
            sp.dma_start(b2t[:, :], b2.rearrange("(p o) -> p o", o=1).broadcast_to([128, 1])).then_inc(setup_c, 16)
            sp.dma_start(bt1[:, :], b_top1.rearrange("(m p) -> p m", p=128),
                         allow_slow_non_contiguous=True).then_inc(setup_c, 16)
            sp.dma_start(bt2[:, :], b_top2.rearrange("(m p) -> p m", p=128),
                         allow_slow_non_contiguous=True).then_inc(setup_c, 16)
            sp.dma_start(wt1[:, :], W_top1[0:128, :]).then_inc(setup_c, 16)
            for bq in range(4):
                sp.dma_start(wta[0:DENSE, bq, :], W_top1[129:145, :]).then_inc(setup_c, 16)
                sp.dma_start(wta[32 + bq:33 + bq, bq, :], W_top1[128:129, :]).then_inc(setup_c, 16)
            sp.dma_start(wt2[:, :, :], W_top2.rearrange("(k p) n -> p k n", p=128)).then_inc(setup_c, 16)
            sp.dma_start(wt3[:, :, :], W_top3.rearrange("(k p) n -> p k n", p=128),
                         allow_slow_non_contiguous=True).then_inc(setup_c, 16)
            sp.dma_start(dense[:, :, :], dense_ctx.rearrange("(g p) c -> p g c", p=128)).then_inc(setup_c, 16)

            with sp.Fori(0, G - 1) as i:
                sp.wait_ge(gathered, (i + 1) * (16 * F))
                load_idx(i + 1)
                sp.wait_ge(xlo_ready, i + 2)
                sp.wait_ge(q_done, i * 2 + 1)
                load_xq(0)
                for c in range(CH):
                    sp.wait_ge(product_ready, (i * CH + c) * NS + (len(L0_SLOTS) + NS))
                    load_piece(c)
                sp.wait_ge(q_done, i * 2 + 2)
                load_xq(1)

            for bq in range(4):
                sp.wait_ge(y_copied, bq + 1)
                sp.dma_start(out.rearrange("(g q r) o -> q o g r", q=4, r=32)[bq],
                             y[0:1, bq, :].rearrange("p (g r) -> p g r", r=32)).then_inc(stored, 16)
            sp.wait_ge(stored, 64)

        @block.gpsimd
        def _(pool):
            def gather(f):
                nc.gpsimd.indirect_dma_start(
                    rows[:, f * D:(f + 1) * D], None, tables[f],
                    bass.IndirectOffsetOnAxis(ap=idx[:, f:f + 1], axis=0)).then_inc(gathered, 16)

            def low_part(x):
                if x.sub == "g":
                    pool.wait_ge(hi_ready, x.hi)
                    nc.gpsimd.tensor_tensor(Plo[:, x.ring, :, :], P[:, x.ring, :, :],
                                            Phi[:, x.ring, :, :].bitcast(F32), ALU.subtract).then_inc(lo_g_ready, 1)

            def chunk(g, c, load_next, last=False):
                if load_next and c == 1:
                    pool.wait_ge(idx_loaded, (g + 2) * 16)
                    pool.wait_ge(x_ready, g + 1)
                for s, x in enumerate(slots_of(g, c, last)):
                    low_part(x)
                    if load_next and 1 <= c <= 4 and s < CH:
                        gather((c - 1) * 8 + s)

            pool.wait_ge(idx_loaded, 16)
            for f in range(F):
                gather(f)
            nc.gpsimd.memset(S[64:128, :, :].bitcast(F32), 0.0).then_inc(zeroed, 1)
            nc.gpsimd.memset(wta[:, :, :], 0.0).then_inc(zeroed, 1)
            nc.gpsimd.memset(aux[:, :, :], 0.0).then_inc(zeroed, 1)
            for s, kind in enumerate(L0_SLOTS):
                low_part(Slot(0, 0, s, kind, prologue=True))
            chunk(0, 0, False)
            with pool.Fori(0, G - 1) as i:
                for c in range(1, CH):
                    chunk(i, c, True)
                chunk(i + 1, 0, False)
            for c in range(1, CH):
                chunk(G - 1, c, False, last=c == CH - 1)

        @block.vector
        def _(dve):
            def product(x):
                dve.wait_ge(bcast_ready, x.done)
                if x.kind == "L1":
                    if x.tile == 0:
                        dve.wait_ge(h0_ready, x.q + 1)
                    other = hdup[:, x.piece % 2, :]
                else:
                    if x.tile == 0 and x.kind == "L0":
                        dve.wait_ge(piece_loaded[x.piece], (x.group + 1) * (16 * PIECE_DMAS))
                    other = xrep[:, x.piece, :]
                if x.kind == "L0x":
                    nc.vector.tensor_tensor(P[:, x.ring, 0, :], pB[:, x.bank, 0, :], other,
                                            ALU.mult).then_inc(product_ready, 1)
                else:
                    nc.vector.tensor_tensor(P[:, x.ring, :, :], pB[:, x.bank, :, :],
                                            other.unsqueeze(1).broadcast_to([128, 2, T]),
                                            ALU.mult).then_inc(product_ready, 1)

            def low_part(x):
                if x is None or x.sub != "v":
                    return
                dve.wait_ge(hi_ready, x.hi)
                if x.kind == "L0x":
                    part = Phi[32:64, x.ring, 0, :]
                    nc.vector.tensor_tensor(part, P[32:64, x.ring, 0, :], part.bitcast(F32),
                                            ALU.subtract).then_inc(lo_v_ready, 1)
                else:
                    nc.vector.tensor_tensor(Plo[:, x.ring, :, :], P[:, x.ring, :, :],
                                            Phi[:, x.ring, :, :].bitcast(F32), ALU.subtract).then_inc(lo_v_ready, 1)

            def h1_low(q):
                dve.wait_ge(h1_ready, q)
                nc.vector.tensor_tensor(h1[H:128, :], h1f[:, :], h1[0:H, :].bitcast(F32),
                                        ALU.subtract).then_inc(h1lo_ready, 1)

            def direct_sum(g, c, q):
                dve.wait_ge(z1_read, q)
                nc.vector.tensor_reduce(
                    feat[:, c % 4, bass.ds(g * 32 + (c // 4) * SB, SB)],
                    direct[:, c % 2, :].rearrange("p (b d) -> p b d", d=D), AX.X, ALU.add).then_inc(direct_used, 1)

            def z2_product(g, half, q):
                dve.wait_ge(v_done, q)
                dve.wait_ge(xq_loaded[half], (g + 1) * 16)
                nc.vector.tensor_tensor(Qp[:, :], pV[:, :], XQ[:, half, :], ALU.mult).then_inc(q_done, 1)

            def z2_turn(n):
                dve.wait_ge(q_done, n)
                nc.vector.transpose(Qt[:, :], Qp[:, :]).then_inc(qt_done, 1)

            def z2_reduce(n):
                dve.wait_ge(qt_done, n)
                nc.vector.tensor_reduce(z2s[:, bass.ds(n - 1, 1), :].rearrange("p o b -> p (o b)"),
                                        Qt[:, :].rearrange("p (b m) -> p b m", m=F), AX.X,
                                        ALU.add).then_inc(z2_sum, 1)

            def turn_rows(g):
                dve.wait_ge(gathered, (g + 1) * (16 * F))
                nc.vector.transpose(X[:, :].rearrange("p (b d) -> p d b", d=D),
                                    rows[:, :].rearrange("p (f d) -> p d f", d=D)).then_inc(x_ready, 1)

            def x_low(g):
                dve.wait_ge(xhi_ready, g + 1)
                nc.vector.tensor_tensor(Xlo[:, :], X[:, :], Xhi[:, :].bitcast(F32),
                                        ALU.subtract).then_inc(xlo_ready, 1)

            def chunk(g, c, load_next, last=False):
                q = CH * g + c
                slots = slots_of(g, c, last)
                first = isinstance(g, int) and g == 0 and c == 0
                for s, x in enumerate(slots):
                    product(x)
                    low_part(back(g, c, s, 1, slots))
                    if s == AT_H1LO and not first:
                        h1_low(q)
                    if s == AT_DIRECT and not first:
                        direct_sum(g if c else g - 1, (c - 1) % CH, q)
                    if c % 4 == 0 and not first:
                        n = 2 * g + c // 4
                        if s == AT_Q:
                            z2_product(g if c else g - 1, (c // 4 + 1) % 2, q)
                        if s == AT_Q + 1:
                            z2_turn(n)
                        if s == AT_Q + 2:
                            z2_reduce(n)
                    if load_next and c == LOAD_C and s == AT_X:
                        for k in range(CH):
                            dve.wait_ge(piece_loaded[k], (g + 1) * (16 * PIECE_DMAS))
                        for half in range(2):
                            dve.wait_ge(xq_loaded[half], (g + 1) * 16)
                        turn_rows(g + 1)
                    if load_next and c == LOAD_C and s == NS - 1:
                        x_low(g + 1)

            dve.wait_ge(setup_w, 16 * 8)
            nc.vector.tensor_copy(ws[:, 0, 0:32], w0s[:, 0:1024:33])
            for s in range(1, 16):
                n = F - s
                dst = ws[:, s // 4, 32 * (s % 4):32 * (s % 4) + 32]
                nc.vector.tensor_tensor(dst[:, 0:n], w0s[:, s:s + 33 * (n - 1) + 1:33],
                                        w0s[:, 32 * s:32 * s + 33 * (n - 1) + 1:33], ALU.add)
                a, b = 1024 - 32 * s, 32 - s
                nc.vector.tensor_tensor(dst[:, n:32], w0s[:, a:a + 33 * (s - 1) + 1:33],
                                        w0s[:, b:b + 33 * (s - 1) + 1:33], ALU.add)
            for r in range(2):
                nc.vector.tensor_copy(ws[:, 4, 32 * r:32 * r + 16], w0s[:, 16:16 + 33 * 15 + 1:33])
                nc.vector.tensor_copy(ws[:, 4, 32 * r + 16:32 * r + 32], w0s[:, 512:512 + 33 * 15 + 1:33])
            nc.vector.memset(ws[:, 4, 64:128], 0.0).then_inc(ws_laid, 1)
            nc.vector.tensor_copy(w1p.rearrange("p (m h) -> p m h", h=H),
                                  w1s.rearrange("p (h m) -> p m h", m=F)).then_inc(w1_laid, 1)
            nc.vector.tensor_copy(Sel[:, :, :].rearrange("p k n -> p (k n)"), selF).then_inc(sel_ready, 1)
            nc.vector.memset(W2p[:, :, :, :].bitcast(F32), 0.0).then_inc(w_lo, 1)
            dve.wait_ge(w_lo, 1)
            for bq in range(4):
                last = nc.vector.tensor_copy(W2p[:, 0, bq, 32 * bq:32 * bq + 32], w2f[:, :])
            last.then_inc(w_lo, 1)
            dve.wait_ge(w_lo, 2)
            for bq in range(4):
                cols = slice(32 * bq, 32 * bq + 32)
                last = nc.vector.tensor_tensor(W2p[:, 1, bq, cols], w2f[:, :], W2p[:, 0, bq, cols].bitcast(F32),
                                               ALU.subtract)
            last.then_inc(w_lo, 1)
            turn_rows(0)
            dve.wait_ge(w_hi, 4)
            nc.vector.tensor_tensor(Wlo[:, 0:4, :], pz0[:, :].rearrange("p (k n) -> p k n", n=128),
                                    Whi[:, 0:4, :].bitcast(F32), ALU.subtract)
            nc.vector.tensor_tensor(Wlo[:, 4, :], pV[:, 0:128], Whi[:, 4, :].bitcast(F32), ALU.subtract)
            nc.vector.tensor_tensor(Wlo[:, 5:N_SEL, :], pB[:, :, :, :].rearrange("p a t (k n) -> p (a t k) n", n=128),
                                    Whi[:, 5:N_SEL, :].bitcast(F32), ALU.subtract).then_inc(w_lo, 1)
            x_low(0)

            slots = [Slot(0, 0, s, kind, prologue=True) for s, kind in enumerate(L0_SLOTS)]
            for x in slots:
                product(x)
                low_part(x)
            chunk(0, 0, False)
            with dve.Fori(0, G - 1) as i:
                for c in range(1, CH):
                    chunk(i, c, True)
                chunk(i + 1, 0, False)
            for c in range(1, CH):
                chunk(G - 1, c, False, last=c == CH - 1)
            low_part(slots_of(G - 1, CH - 1, True)[-1])
            h1_low(NQ)
            direct_sum(G - 1, CH - 1, NQ)
            z2_product(G - 1, 1, NQ)
            z2_turn(2 * G)
            z2_reduce(2 * G)

        @block.scalar
        def _(act):
            def high_part(x):
                if x.sub == "":
                    return
                act.wait_ge(product_ready, x.done)
                if x.kind == "L0x":
                    nc.scalar.copy(Phi[:, x.ring, 0, :], P[:, x.ring, 0, :]).then_inc(hi_ready, 1)
                else:
                    nc.scalar.copy(Phi[:, x.ring, :, :], P[:, x.ring, :, :]).then_inc(hi_ready, 1)

            def z1_out(c, q, main):
                act.wait_ge(main_done, main)
                if not isinstance(q, int) or q > 1:
                    act.wait_ge(v_done, q - 1)
                z = pz1[:, c % 2, :]
                nc.scalar.activation(h1[0:H, :], z[0:H, :], ACT.Relu, bias=b1t[0:H, :])
                nc.scalar.activation(h1f[:, :], z[0:H, :], ACT.Relu, bias=b1t[0:H, :]).then_inc(h1_ready, 1)
                nc.scalar.activation(direct[H:128, c % 2, :], z[H:128, :], ACT.Relu,
                                     bias=b1t[H:128, :]).then_inc(z1_read, 1)

            def z0_out(c, main, used):
                act.wait_ge(main_done, main)
                nc.scalar.activation(hdup[0:H, c % 2, :], pz0[0:H, :], ACT.Relu, bias=b0t[0:H, :])
                nc.scalar.activation(hdup[H:128, c % 2, :], pz0[0:H, :], ACT.Relu,
                                     bias=b0t[0:H, :]).then_inc(h0_ready, 1)
                if used is not None:
                    act.wait_ge(direct_used, used)
                nc.scalar.activation(direct[0:H, c % 2, :], pz0[H:128, :], ACT.Relu,
                                     bias=b0t[H:128, :]).then_inc(z0_read, 1)

            def chunk(g, c, load_next, last=False):
                q = CH * g + c
                first = isinstance(g, int) and g == 0 and c == 0
                for s, x in enumerate(slots_of(g, c, last)):
                    high_part(x)
                    if s == AT_Z1 and not first:
                        z1_out((c - 1) % CH, q, q * NS + len(L0_SLOTS))
                    if s == AT_Z0 and not last:
                        if not first:
                            act.wait_ge(product_ready, q * NS + len(L0_SLOTS))
                        z0_out((c + 1) % CH, q * NS + (len(L0_SLOTS) + L0X_AT + 1), None if first else q)
                    if load_next and c == LOAD_C and s == AT_X + 1:
                        act.wait_ge(x_ready, g + 2)
                        nc.scalar.copy(Xhi[:, :], X[:, :]).then_inc(xhi_ready, 1)

            act.wait_ge(x_ready, 1)
            nc.scalar.copy(Xhi[:, :], X[:, :]).then_inc(xhi_ready, 1)
            act.wait_ge(w_turned, 3)
            turned = [(slice(0, 4), pz0[:, :].rearrange("p (k n) -> p k n", n=128)),
                      (slice(4, 5), pV[:, 0:128].rearrange("p (k n) -> p k n", n=128)),
                      (slice(5, 13), pB[:, 0, :, :].rearrange("p t (k n) -> p (t k) n", n=128)),
                      (slice(13, 21), pB[:, 1, :, :].rearrange("p t (k n) -> p (t k) n", n=128))]
            for k, psum in turned:
                if Wf is not None:
                    nc.scalar.copy(Wf[:, k, :], psum)
                nc.scalar.copy(Whi[:, k, :], psum).then_inc(w_hi, 1)

            for s, kind in enumerate(L0_SLOTS):
                high_part(Slot(0, 0, s, kind, prologue=True))
            z0_out(0, len(L0_SLOTS), None)
            chunk(0, 0, False)
            with act.Fori(0, G - 1) as i:
                for c in range(1, CH):
                    chunk(i, c, True)
                chunk(i + 1, 0, False)
            for c in range(1, CH):
                chunk(G - 1, c, False, last=c == CH - 1)
            z1_out(CH - 1, NQ, slots_of(G - 1, CH - 1, True)[-1].done)

            act.wait_ge(setup_c, 16 * 16)
            act.wait_ge(zeroed, 3)
            act.wait_ge(dense_turned, 1)
            nc.scalar.copy(aux[0:DENSE, :, :].rearrange("p q (g r) -> p q g r", r=32),
                           pB[0:DENSE, :, :, :].rearrange("p a t (g q r) -> p q (a t g) r", q=4, r=32))
            act.wait_ge(z2_sum, 2 * G)
            nc.scalar.activation(z2r[:, :], z2s[:, :, :].rearrange("p g b -> p (g b)"), ACT.Relu,
                                 bias=b2t[:, :]).then_inc(z2_relu, 1)
            act.wait_ge(z2_row, 1)
            nc.scalar.copy(aux[32:36, :, :], pV[0:4, :].unsqueeze(1).broadcast_to([4, 4, T])).then_inc(aux_ready, 1)

            def hid1_out(bq):
                for m in range(4):
                    act.wait_ge(hid1_done, 4 * bq + m + 1)
                    if bq >= 2 and m == 0:
                        act.wait_ge(hid2_done, 2 * (bq - 1))
                    nc.scalar.activation(hid1[:, bq % 2, m, :], pB[:, m // 2, m % 2, :], ACT.Relu,
                                         bias=bt1[:, m:m + 1]).then_inc(hid1_act, 1)

            def hid2_out(bq):
                for m in range(2):
                    act.wait_ge(hid2_done, 2 * bq + m + 1)
                    if bq >= 2 and m == 0:
                        act.wait_ge(y_done, bq - 1)
                    nc.scalar.activation(hid2[:, bq % 2, m, :], pz1[:, m, :], ACT.Relu,
                                         bias=bt2[:, m:m + 1]).then_inc(hid2_act, 1)

            hid1_out(0)
            for bq in range(4):
                if bq < 3:
                    hid1_out(bq + 1)
                hid2_out(bq)
                act.wait_ge(y_done, bq + 1)
                nc.scalar.copy(y[0:1, bq, :], pz0[0:1, :]).then_inc(y_copied, 1)

        @block.tensor
        def _(pe):
            def broadcast(x):
                if not isinstance(x.done, int) or x.done > 2:
                    pe.wait_ge(product_ready, x.done - 2)
                if x.kind == "L0" and x.tile == 0:
                    pe.wait_ge(piece_loaded[x.piece], (x.group + 1) * (16 * PIECE_DMAS))
                first, n = {"L0": (2 * x.tile, 2), "L0x": (4, 1), "L1": (5 + 2 * x.tile, 2)}[x.kind]
                for t in range(n):
                    last = nc.tensor.matmul(pB[:, x.bank, t, :], Sel[:, first + t, :], S[:, x.piece, :],
                                            start=True, stop=True)
                last.then_inc(bcast_ready, 1)

            def main(x):
                if x.sub == "v":
                    pe.wait_ge(lo_v_ready, x.lo_v)
                elif x.sub == "g":
                    pe.wait_ge(lo_g_ready, x.lo_g)
                else:
                    pe.wait_ge(product_ready, x.done)
                if x.kind == "L0x":
                    if x.sub:
                        nc.tensor.matmul(pz0[:, :], Wlo[:, 4, :], Phi[:, x.ring, 0, :], start=False, stop=False)
                        last = nc.tensor.matmul(pz0[:, :], Whi[:, 4, :], Phi[:, x.ring, 0, :], start=False, stop=True)
                    else:
                        last = nc.tensor.matmul(pz0[:, :], Wf[0:32, 4, :], P[0:32, x.ring, 0, :],
                                                start=False, stop=True)
                    last.then_inc(main_done, 1)
                    return
                if x.kind == "L0":
                    acc, first, opens, closes = pz0[:, :], 2 * x.tile, x.tile == 0, False
                    if opens and not (isinstance(x.q, int) and x.q == 0):
                        pe.wait_ge(z0_read, x.q)
                else:
                    acc, first, opens, closes = pz1[:, x.piece % 2, :], 5 + 2 * x.tile, x.tile == 0, x.tile == 7
                    if opens and not (isinstance(x.q, int) and x.q < 2):
                        pe.wait_ge(z1_read, x.q - 1)
                for t in range(2):
                    if x.sub:
                        hi, lo = Phi[:, x.ring, t, :], Plo[:, x.ring, t, :]
                        nc.tensor.matmul(acc, Wlo[:, first + t, :], hi, start=opens and t == 0, stop=False)
                        nc.tensor.matmul(acc, Whi[:, first + t, :], hi, start=False, stop=False)
                        last = nc.tensor.matmul(acc, Whi[:, first + t, :], lo, start=False, stop=closes and t == 1)
                    else:
                        last = nc.tensor.matmul(acc, Wf[:, first + t, :], P[:, x.ring, t, :],
                                                start=opens and t == 0, stop=closes and t == 1)
                last.then_inc(main_done, 1)

            def layer2(g, c, q):
                pe.wait_ge(h1lo_ready, q)
                if c % 4 == 0 and not (isinstance(g, int) and g == 0 and c == 0):
                    pe.wait_ge(q_done, 2 * g + c // 4)
                nc.tensor.matmul(pV[:, :], W2p[:, 1, c % 4, :], h1[:, :], start=c % 4 == 0, stop=False)
                nc.tensor.matmul(pV[:, :], W2p[:, 0, c % 4, :], h1[:, :], start=False,
                                 stop=c % 4 == 3).then_inc(v_done, 1)

            def chunk(g, c, last=False):
                q = CH * g + c
                slots = slots_of(g, c, last)
                first = isinstance(g, int) and g == 0 and c == 0
                for s, x in enumerate(slots):
                    broadcast(x)
                    behind = back(g, c, s, LAG, slots)
                    if behind is not None:
                        main(behind)
                    if s == AT_V and not first:
                        layer2(g if c else g - 1, (c - 1) % CH, q)

            pe.wait_ge(setup_w, 16 * 8)
            pe.wait_ge(ws_laid, 1)
            for k in range(L0_TILES):
                last = nc.tensor.transpose(pz0[:, 128 * k:128 * k + 128], ws[:, k, :], ident[:, :])
            last.then_inc(w_turned, 1)
            nc.tensor.transpose(pV[:, 0:128], ws[:, 4, :], ident[:, :]).then_inc(w_turned, 1)
            pe.wait_ge(w1_laid, 1)
            for k in range(L1_TILES):
                last = nc.tensor.transpose(pB[:, k // 8, (k // 4) % 2, 128 * (k % 4):128 * (k % 4) + 128],
                                           w1p[:, 128 * k:128 * k + 128], ident[:, :])
            last.then_inc(w_turned, 1)
            pe.wait_ge(w_lo, 4)
            pe.wait_ge(sel_ready, 1)
            pe.wait_ge(zeroed, 1)

            slots = [Slot(0, 0, s, kind, prologue=True) for s, kind in enumerate(L0_SLOTS)]
            for x in slots:
                broadcast(x)
            for x in slots:
                main(x)
            chunk(0, 0)
            with pe.Fori(0, G - 1) as i:
                for c in range(1, CH):
                    chunk(i, c)
                chunk(i + 1, 0)
            for c in range(1, CH):
                chunk(G - 1, c, last=c == CH - 1)
            for x in slots_of(G - 1, CH - 1, True)[-LAG:]:
                main(x)

            pe.wait_ge(product_ready, slots_of(G - 1, CH - 1, True)[-1].done)
            pe.wait_ge(setup_c, 16 * 16)
            for g in range(G):
                last = nc.tensor.transpose(pB[0:DENSE, g // 8, (g // 4) % 2, 128 * (g % 4):128 * (g % 4) + 128],
                                           dense[:, g, :], ident[:, :])
            last.then_inc(dense_turned, 1)
            layer2(G - 1, CH - 1, NQ)
            pe.wait_ge(z2_relu, 1)
            nc.tensor.matmul(pV[0:4, :], ones4[:, :], z2r[:, :], start=True, stop=True).then_inc(z2_row, 1)
            pe.wait_ge(aux_ready, 1)
            pe.wait_ge(direct_used, NQ)

            def to_hid1(bq):
                for m in range(4):
                    cols = slice(128 * m, 128 * m + 128)
                    bank = pB[:, m // 2, m % 2, :]
                    if bq >= 1:
                        pe.wait_ge(hid1_act, 4 * (bq - 1) + m + 1)
                    nc.tensor.matmul(bank, wt1[:, cols], feat[:, bq, :], start=True, stop=False)
                    nc.tensor.matmul(bank, wta[:, bq, cols], aux[:, bq, :], start=False,
                                     stop=True).then_inc(hid1_done, 1)

            def to_hid2(bq):
                for m in range(2):
                    if m == 0:
                        pe.wait_ge(hid1_act, 4 * bq + 4)
                    if bq >= 1:
                        pe.wait_ge(hid2_act, 2 * (bq - 1) + m + 1)
                    for k in range(4):
                        last = nc.tensor.matmul(pz1[:, m, :], wt2[:, k, 128 * m:128 * m + 128],
                                                hid1[:, bq % 2, k, :], start=k == 0, stop=k == 3)
                    last.then_inc(hid2_done, 1)

            def to_y(bq):
                pe.wait_ge(hid2_act, 2 * bq + 2)
                if bq >= 1:
                    pe.wait_ge(y_copied, bq)
                for k in range(2):
                    last = nc.tensor.matmul(pz0[0:1, :], wt3[:, k, :], hid2[:, bq % 2, k, :],
                                            start=k == 0, stop=k == 1)
                last.then_inc(y_done, 1)

            to_hid1(0)
            for bq in range(4):
                if bq < 3:
                    to_hid1(bq + 1)
                to_hid2(bq)
                to_y(bq)


_FLOATS = ["dense_ctx", "ids", "W_top1", "b_top1", "W_top2", "b_top2", "W_top3",
           "L0_rec_W0", "L0_rec_b0", "L0_rec_W1", "L0_rec_b1", "L0_rec_W2", "L0_rec_b2"]


def _constants():
    import numpy as np

    sel = np.zeros((128, N_SEL, 128), np.float32)
    for part in (0, 32):
        for t in range(L0_TILES):
            for j in range(128):
                sel[part + (j % 32 + 4 * t + j // 32) % 32, t, j] = 1
        for j in range(64):
            sel[part + (j % 32 + 16) % 32, L0_TILES, j] = 1
        for k in range(L1_TILES):
            for j in range(128):
                sel[part + 2 * k + j // 64, L0_TILES + 1 + k, j] = 1
    ones = np.zeros((128, 4), np.float32)
    for q in range(4):
        ones[32 * q:32 * q + 32, q] = 1
    return {"sel": sel.reshape(128, -1), "ident": np.eye(128, dtype=np.float32), "ones": ones}


def kernel(**inputs):
    import numpy as np
    import concourse.bacc as bacc
    from concourse.bass_utils import run_bass_kernel_spmd

    nc = bacc.Bacc("TRN2", target_bir_lowering=False, num_devices=1)
    arrays = {}

    def dram(name, a):
        arrays[name] = np.ascontiguousarray(a)
        return nc.dram_tensor(name, a.shape, mybir.dt.from_np(a.dtype), kind="ExternalInput").ap()

    tables = [dram(f"tbl_{f}", np.asarray(inputs[f"tbl_{f}"])) for f in range(F)]
    args = [dram("in_" + n, np.asarray(inputs[n])) for n in _FLOATS]
    consts = [dram("c_" + n, a) for n, a in _constants().items()]
    out = nc.dram_tensor("y_out", (B, 1), F32, kind="ExternalOutput").ap()
    build(nc, tables, *args, *consts, out)
    r = run_bass_kernel_spmd(nc, [arrays], core_ids=[0])
    return r.results[0]["y_out"]
```

```python
import concourse.bass as bass
from concourse import mybir
from contextlib import ExitStack

F32 = mybir.dt.float32
F32R = mybir.dt.float32r
I32 = mybir.dt.int32
ALU = mybir.AluOpType
ACT = mybir.ActivationFunctionType
AX = mybir.AxisListType

B, F, D = 2048, 32, 32
O = 128
H = O // 2
DENSE, HID1, HID2 = 16, 512, 256
G = B // 128
CH = 8
T = 512
SB = T // D
NQ = G * CH
L0_TILES = 4
L1_TILES = 16
N_TILES = L0_TILES + 1 + L1_TILES
LAG = 5
P_RING, PG_RING, PART_RING, BX_RING = 3, 4, 7, 2
LOW_BACK = 2
PIECE_DMAS = 2

L0_STREAM = [("L0", 0, "v", True), ("L0", 1, "v", True), ("L0x", 0, "v", True)]
STREAM = [("L0", 0, "v", True), ("L1", 0, "g", False), ("L0", 1, "v", True), ("L1", 1, "g", True),
          ("L0x", 0, "v", True), ("L1", 2, "g", False), ("L1", 3, "v", True), ("L1", 4, "g", True),
          ("L1", 5, "v", True), ("L1", 6, "g", False), ("L1", 7, "v", True)]
LAST_STREAM = [k for k in STREAM if k[0] == "L1"]
WHOLE_TILES = [L0_TILES + 1 + 2 * k[1] + t for k in STREAM if not k[3] for t in range(2)]
SEL_TILES = list(range(L0_TILES + 1)) + [L0_TILES + 1 + 2 * k[1] + t for k in STREAM
                                         if k[0] == "L1" and k[2] == "v" for t in range(2)]
NS, N0 = len(STREAM), len(L0_STREAM)
L0X_AT = STREAM.index(L0_STREAM[-1])
AT_Z1 = LAG - 1
AT_Z0 = L0X_AT + LAG
AT_H1LO = 6
AT_DIRECT = 7
AT_V = 8
AT_Q = 9
GATHER_S, GATHER_STEP = 3, 2
HEAD_C = 3
LOAD_C = 6
AT_X = 1
AT_XHI = 2
AT_XLO = 4
LOAD_AT = {(6, 6): 0, (6, 8): 1, (6, 10): 2, (7, 1): 3, (7, 3): 4, (7, 5): 5, (7, 7): 6, (0, 2): 7}
LOAD_XQ_AT = {(7, 9): 0, (1, 1): 1}


def is_made(by):
    return lambda k: k[2] == by


def is_split(k):
    return k[3]


def is_pair(k):
    return k[3] and k[0] != "L0x"


class Slot:

    def __init__(self, g, c, s, stream, prologue=False):
        self.kind, self.tile, self.maker, self.split = stream[s]
        before = L0_STREAM[:s + 1] if prologue else L0_STREAM + STREAM * c + stream[:s + 1]

        def count(which):
            return sum(map(which, before))

        def over_groups(which):
            return count(which) if prologue else g * sum(map(which, STREAM * CH)) + count(which)

        def before_in_ring(which, ring, of=bool):
            known = before if isinstance(g, int) and g == 0 else STREAM * 2 + before[N0:]
            at = [i for i, k in enumerate(known) if which(k)]
            if len(at) <= ring:
                return None
            return over_groups(of) - sum(map(of, known[at[-1 - ring] + 1:at[-1] + 1]))

        self.done = over_groups(bool)
        self.made_v, self.made_g = over_groups(is_made("v")), over_groups(is_made("g"))
        self.parts = over_groups(is_split)
        if self.maker == "v":
            self.bank = (count(is_made("v")) - 1) % 2
            self.p = (count(is_made("v")) - 1) % P_RING
            self.p_free = before_in_ring(is_made("v"), P_RING, is_split)
        else:
            n = count(is_made("g"))
            self.p = (n - 1) % PG_RING
            self.p_free = before_in_ring(is_made("g"), PG_RING)
            self.bx = (n - 1) % BX_RING
            self.bx_uses = g * (sum(map(is_made("g"), STREAM * CH)) // BX_RING) + (n - 1) // BX_RING + 1
            self.bx_free = self.made_g - BX_RING if self.p_free is not None or n > BX_RING else None
        if is_pair(stream[s]):
            self.part = (count(is_pair) - 1) % PART_RING
            self.part_free = before_in_ring(is_pair, PART_RING)
        q = CH * g + c
        if self.kind == "L1":
            self.piece, self.q = c, q
        elif prologue:
            self.piece, self.q, self.group = 0, 0, 0
        else:
            self.piece, self.q = (c + 1) % CH, q + 1
            self.group = g + (c + 1) // CH


assert all(sum(map(which, STREAM)) * CH % ring == 0
           for which, ring in ((is_made("v"), P_RING), (is_made("v"), 2), (is_made("g"), PG_RING),
                               (is_made("g"), BX_RING), (is_pair, PART_RING)))
assert all(k[0] == "L1" if k[2] == "g" else k[3] for k in STREAM)
MADE_V, MADE_G = sum(map(is_made("v"), STREAM)), sum(map(is_made("g"), STREAM))


def slots_of(g, c, last=False):
    stream = LAST_STREAM if last else STREAM
    return [Slot(g, c, s, stream) for s in range(len(stream))]


def prologue_slots():
    return [Slot(0, 0, s, L0_STREAM, prologue=True) for s in range(N0)]


def back(g, c, s, k, slots):
    if s >= k:
        return slots[s - k]
    if c == 0 and isinstance(g, int) and g == 0:
        return None
    return slots_of(g - 1 if c == 0 else g, (c - 1) % CH)[s - k]


def build(nc, tables, dense_ctx, ids, W_top1, b_top1, W_top2, b_top2, W_top3, W0, b0, W1, b1, W2, b2,
          sel_c, ident_c, ones_c, out):
    ctx = ExitStack()
    with ctx:
        def sb(name, shape, dt=F32):
            return ctx.enter_context(nc.sbuf_tensor(name, shape, dt))

        def ps(name, shape):
            return ctx.enter_context(nc.psum_tensor(name, shape, F32))

        def sem(name):
            return ctx.enter_context(nc.semaphore(name))

        idx = sb("idx", [128, F], I32)
        rows = sb("rows", [128, F * D])
        X = sb("X", [128, 2 * T])
        Xparts = sb("Xparts", [128, 2, 2 * T], F32R)
        S = sb("S", [128, CH, T], F32R)
        xrep = sb("xrep", [128, CH, T])
        XQ = sb("XQ", [128, 2, T])
        BX = sb("BX", [128, BX_RING, 2, T])
        P = sb("P", [128, P_RING, 2, T])
        Pg = sb("Pg", [128, PG_RING, 2, T])
        Phi = sb("Phi", [128, PART_RING, 2, T], F32R)
        Plo = sb("Plo", [128, PART_RING, 2, T], F32R)
        Pxparts = sb("Pxparts", [128, T], F32R)
        outs = sb("outs", [128, 4, T])
        hdup = outs[:, 0:2, :]
        direct = outs[:, 2:4, :]
        h1f = sb("h1f", [H, T])
        h1 = sb("h1", [128, T], F32R)
        Qp = sb("Qp", [128, T])
        Qt = sb("Qt", [128, T])
        z2s = sb("z2s", [128, G * 2, SB])
        feat = sb("feat", [128, 4, G * 2 * SB])
        Sel = sb("Sel", [128, len(SEL_TILES), 128], F32R)
        Whi = sb("Whi", [128, N_TILES, 128], F32R)
        Wlo = sb("Wlo", [128, N_TILES, 128], F32R)
        Wf = sb("Wf", [128, len(WHOLE_TILES), 128])
        w2f = sb("w2f", [128, F])
        W2p = sb("W2p", [128, 2, 4, 128], F32R)
        ident = sb("ident", [128, 128])
        ones4 = sb("ones4", [128, 4])
        b0t, b1t, b2t = sb("b0t", [128, 1]), sb("b1t", [128, 1]), sb("b2t", [128, 1])
        bt1, bt2 = sb("bt1", [128, 4]), sb("bt2", [128, 2])
        wt1 = X[:, 0:HID1]
        wt2 = rows[:, :].rearrange("p (k n) -> p k n", k=4)
        wta = Xparts[0:36, :, :].bitcast(F32).rearrange("p a (e n) -> p (a e) n", n=HID1)
        wt3 = sb("wt3", [128, 2, 1])
        dense = sb("dense", [128, G, DENSE])
        w1s = Pg[:, 0:2, :, :].rearrange("p r t n -> p (r t n)")
        w1p = Pg[:, 2:4, :, :].rearrange("p r t n -> p (r t n)")
        flat = xrep[:, :, :].rearrange("p c n -> p (c n)")
        selF = flat[:, 0:len(SEL_TILES) * 128]
        w0s = flat[:, 3072:4096]
        ws = P[:, 0, :, :].rearrange("p t n -> p (t n)")[:, 0:5 * 128].rearrange("p (k n) -> p k n", k=5)
        z2r = Qt
        aux = outs[0:36, :, :]
        hid1 = Pg[:, :, :, :].rearrange("p (e r) t n -> p e (r t) n", e=2)
        hid2 = xrep[:, 0:4, :].rearrange("p (e m) n -> p e m n", e=2)
        y = xrep[0:1, 4:8, :]

        pB = ps("pB", [128, 2, 2, T])
        pz0 = ps("pz0", [128, T])
        pz1 = ps("pz1", [128, 2, T])
        pV = ps("pV", [128, T])

        setup_w = sem("setup_w")
        setup_c = sem("setup_c")
        idx_loaded = sem("idx_loaded")
        gathered = sem("gathered")
        zeroed = sem("zeroed")
        w1_laid = sem("w1_laid")
        ws_zero = sem("ws_zero")
        ws_laid = sem("ws_laid")
        w_turned = sem("w_turned")
        w_hi = sem("w_hi")
        w_lo = sem("w_lo")
        sel_ready = sem("sel_ready")
        x_ready = sem("x_ready")
        xhi_ready = sem("xhi_ready")
        xlo_ready = sem("xlo_ready")
        piece_loaded = [sem(f"piece_loaded{c}") for c in range(CH)]
        xq_loaded = [sem(f"xq_loaded{h}") for h in range(2)]
        bcast_ready = sem("bcast_ready")
        made_v = sem("made_v")
        made_g = sem("made_g")
        bx_loaded = [sem(f"bx_loaded{r}") for r in range(BX_RING)]
        hi_ready = sem("hi_ready")
        lo_ready = sem("lo_ready")
        main_done = sem("main_done")
        h0_ready = sem("h0_ready")
        z0_read = sem("z0_read")
        h1_ready = sem("h1_ready")
        h1lo_ready = sem("h1lo_ready")
        z1_read = sem("z1_read")
        direct_used = sem("direct_used")
        v_done = sem("v_done")
        q_done = sem("q_done")
        qt_done = sem("qt_done")
        z2_sum = sem("z2_sum")
        z2_relu = sem("z2_relu")
        z2_row = sem("z2_row")
        dense_turned = sem("dense_turned")
        aux_ready = sem("aux_ready")
        hid1_done, hid1_act = sem("hid1_done"), sem("hid1_act")
        hid2_done, hid2_act = sem("hid2_done"), sem("hid2_act")
        y_done, y_copied, stored = sem("y_done"), sem("y_copied"), sem("stored")

        ids_g = ids.rearrange("(g p) f -> g p f", p=128)
        block = ctx.enter_context(nc.Block())

        @block.sync
        def _(sp):
            def load_idx(g):
                sp.dma_start(idx[:, :], ids_g[g]).then_inc(idx_loaded, 16)

            def chunk(g, c, load_next, last=False):
                for x in [x for x in slots_of(g, c, last) if x.maker == "g"]:
                    if x.bx_free is not None:
                        sp.wait_ge(made_g, x.bx_free)
                    if x.tile == 0:
                        if load_next and c == 0:
                            sp.wait_ge(gathered, (g + 1) * (16 * F))
                            load_idx(g + 1)
                        sp.wait_ge(piece_loaded[c], (g + 1) * (16 * PIECE_DMAS))
                    for t in range(2):
                        k = 2 * x.tile + t
                        sp.dma_start(BX[:, x.bx, t, :], xrep[8 * k:8 * k + 8, c, :].unsqueeze(1)
                                     .broadcast_to([8, 16, T])).then_inc(bx_loaded[x.bx], 16)

            load_idx(0)
            sp.dma_start(w0s, W0).then_inc(setup_w, 16)
            sp.dma_start(ident[:, :], ident_c).then_inc(setup_w, 16)
            sp.dma_start(w1s, W1).then_inc(setup_w, 16)
            sp.dma_start(w2f[0:H, :], W2.rearrange("o (h m) -> (o h) m", m=F)).then_inc(setup_w, 16)
            sp.dma_start(w2f[H:128, :], W2.rearrange("o (h m) -> (o h) m", m=F)).then_inc(setup_w, 16)
            sp.dma_start(selF, sel_c).then_inc(setup_w, 16)
            sp.dma_start(b0t[:, :], b0.rearrange("(p o) -> p o", o=1)).then_inc(setup_w, 16)
            sp.dma_start(b1t[:, :], b1.rearrange("(p o) -> p o", o=1)).then_inc(setup_w, 16)
            sp.dma_start(ones4[:, :], ones_c).then_inc(setup_c, 16)
            sp.dma_start(b2t[:, :], b2.rearrange("(p o) -> p o", o=1).broadcast_to([128, 1])).then_inc(setup_c, 16)
            sp.dma_start(bt1[:, :], b_top1.rearrange("(m p) -> p m", p=128),
                         allow_slow_non_contiguous=True).then_inc(setup_c, 16)
            sp.dma_start(bt2[:, :], b_top2.rearrange("(m p) -> p m", p=128),
                         allow_slow_non_contiguous=True).then_inc(setup_c, 16)
            sp.dma_start(wt3[:, :, :], W_top3.rearrange("(k p) n -> p k n", p=128),
                         allow_slow_non_contiguous=True).then_inc(setup_c, 16)
            sp.dma_start(dense[:, :, :], dense_ctx.rearrange("(g p) c -> p g c", p=128)).then_inc(setup_c, 16)

            for c in range(CH):
                chunk(0, c, True)
            with sp.Fori(1, G - 1) as i:
                for c in range(CH):
                    chunk(i, c, True)
            for c in range(CH):
                if c == HEAD_C:
                    sp.wait_ge(zeroed, 2)
                    sp.dma_start(wt1[:, :], W_top1[0:128, :]).then_inc(setup_c, 16)
                    for bq in range(4):
                        sp.dma_start(wta[0:DENSE, bq, :], W_top1[129:145, :]).then_inc(setup_c, 16)
                        sp.dma_start(wta[32 + bq:33 + bq, bq, :], W_top1[128:129, :]).then_inc(setup_c, 16)
                    sp.dma_start(wt2[:, :, :], W_top2.rearrange("(k p) n -> p k n", p=128)).then_inc(setup_c, 16)
                chunk(G - 1, c, False, last=c == CH - 1)

            for bq in range(4):
                sp.wait_ge(y_copied, bq + 1)
                sp.dma_start(out.rearrange("(g q r) o -> q o g r", q=4, r=32)[bq],
                             y[0:1, bq, :].rearrange("p (g r) -> p g r", r=32)).then_inc(stored, 16)
            sp.wait_ge(stored, 64)

        @block.gpsimd
        def _(pool):
            def gather(f):
                nc.gpsimd.indirect_dma_start(
                    rows[:, f * D:(f + 1) * D], None, tables[f],
                    bass.IndirectOffsetOnAxis(ap=idx[:, f:f + 1], axis=0)).then_inc(gathered, 16)

            def product(x):
                if x.maker != "g":
                    return
                if x.tile == 0:
                    pool.wait_ge(h0_ready, x.q + 1)
                if x.p_free is not None:
                    pool.wait_ge(main_done, x.p_free)
                pool.wait_ge(bx_loaded[x.bx], x.bx_uses * 32)
                nc.gpsimd.tensor_tensor(Pg[:, x.p, :, :], BX[:, x.bx, :, :],
                                        hdup[:, x.piece % 2, :].unsqueeze(1).broadcast_to([128, 2, T]),
                                        ALU.mult).then_inc(made_g, 1)

            def chunk(g, c, load_next, last=False):
                for s, x in enumerate(slots_of(g, c, last)):
                    f, off = divmod(c * NS + s - GATHER_S, GATHER_STEP)
                    if load_next and (f, off) == (0, 0):
                        pool.wait_ge(idx_loaded, (g + 2) * 16)
                        pool.wait_ge(x_ready, g + 1)
                    product(x)
                    if load_next and off == 0 and 0 <= f < F:
                        gather(f)

            pool.wait_ge(idx_loaded, 16)
            for f in range(F):
                gather(f)
            nc.gpsimd.memset(S[64:128, :, :].bitcast(F32), 0.0).then_inc(zeroed, 1)
            for c in range(CH):
                chunk(0, c, True)
            with pool.Fori(1, G - 1) as i:
                for c in range(CH):
                    chunk(i, c, True)
            for c in range(CH):
                if c == HEAD_C:
                    for k in range(CH):
                        pool.wait_ge(piece_loaded[k], G * (16 * PIECE_DMAS))
                    for half in range(2):
                        pool.wait_ge(xq_loaded[half], G * 16)
                    nc.gpsimd.memset(wta, 0.0).then_inc(zeroed, 1)
                chunk(G - 1, c, False, last=c == CH - 1)

        @block.vector
        def _(dve):
            def product(x):
                if x.maker != "v":
                    return
                if x.p_free is not None:
                    dve.wait_ge(lo_ready, x.p_free)
                dve.wait_ge(bcast_ready, x.made_v)
                if x.kind == "L1":
                    dve.wait_ge(h0_ready, x.q + 1)
                    other = hdup[:, x.piece % 2, :]
                else:
                    dve.wait_ge(piece_loaded[x.piece], (x.group + 1) * (16 * PIECE_DMAS))
                    other = xrep[:, x.piece, :]
                if x.kind == "L0x":
                    nc.vector.tensor_tensor(P[:, x.p, 0, :], pB[:, x.bank, 0, :], other,
                                            ALU.mult).then_inc(made_v, 1)
                else:
                    nc.vector.tensor_tensor(P[:, x.p, :, :], pB[:, x.bank, :, :],
                                            other.unsqueeze(1).broadcast_to([128, 2, T]),
                                            ALU.mult).then_inc(made_v, 1)

            def low_part(x):
                if x is None or not x.split:
                    return
                dve.wait_ge(hi_ready, x.parts)
                if x.kind == "L0x":
                    part = Pxparts[64:128, :]
                    nc.vector.tensor_tensor(part, P[64:128, x.p, 0, :], part.bitcast(F32),
                                            ALU.subtract).then_inc(lo_ready, 1)
                else:
                    made = P if x.maker == "v" else Pg
                    nc.vector.tensor_tensor(Plo[:, x.part, :, :], made[:, x.p, :, :],
                                            Phi[:, x.part, :, :].bitcast(F32), ALU.subtract).then_inc(lo_ready, 1)

            def h1_low(q):
                dve.wait_ge(h1_ready, q)
                nc.vector.tensor_tensor(h1[H:128, :], h1f[:, :], h1[0:H, :].bitcast(F32),
                                        ALU.subtract).then_inc(h1lo_ready, 1)

            def direct_sum(g, c, q):
                dve.wait_ge(z1_read, q)
                nc.vector.tensor_reduce(
                    feat[:, c % 4, bass.ds(g * 32 + (c // 4) * SB, SB)],
                    direct[:, c % 2, :].rearrange("p (b d) -> p b d", d=D), AX.X, ALU.add).then_inc(direct_used, 1)

            def z2_product(g, half, q):
                dve.wait_ge(v_done, q)
                dve.wait_ge(xq_loaded[half], (g + 1) * 16)
                nc.vector.tensor_tensor(Qp[:, :], pV[:, :], XQ[:, half, :], ALU.mult).then_inc(q_done, 1)

            def z2_turn(n):
                dve.wait_ge(q_done, n)
                nc.vector.transpose(Qt[:, :], Qp[:, :]).then_inc(qt_done, 1)

            def z2_reduce(n):
                dve.wait_ge(qt_done, n)
                nc.vector.tensor_reduce(z2s[:, bass.ds(n - 1, 1), :].rearrange("p o b -> p (o b)"),
                                        Qt[:, :].rearrange("p (b m) -> p b m", m=F), AX.X,
                                        ALU.add).then_inc(z2_sum, 1)

            def turn_rows(g):
                dve.wait_ge(gathered, (g + 1) * (16 * F))
                nc.vector.transpose(X[:, :].rearrange("p (b d) -> p d b", d=D),
                                    rows[:, :].rearrange("p (f d) -> p d f", d=D)).then_inc(x_ready, 1)

            def x_low(g):
                dve.wait_ge(xhi_ready, g + 1)
                nc.vector.tensor_tensor(Xparts[:, 1, :], X[:, :], Xparts[:, 0, :].bitcast(F32),
                                        ALU.subtract).then_inc(xlo_ready, 1)

            def chunk(g, c, load_next, last=False):
                q = CH * g + c
                slots = slots_of(g, c, last)
                first = isinstance(g, int) and g == 0 and c == 0
                for s, x in enumerate(slots):
                    product(x)
                    turn = c % 4 == 0 and not first and s == AT_Q + 1
                    n = 2 * g + c // 4
                    if turn:
                        z2_turn(n)
                    low_part(back(g, c, s, LOW_BACK, slots))
                    if turn:
                        z2_reduce(n)
                    if s == AT_H1LO and not first:
                        h1_low(q)
                    if s == AT_DIRECT and not first:
                        direct_sum(g if c else g - 1, (c - 1) % CH, q)
                    if c % 4 == 0 and not first and s == AT_Q:
                        z2_product(g if c else g - 1, (c // 4 + 1) % 2, q)
                    if load_next and c == LOAD_C and s == AT_X:
                        for k in range(CH):
                            dve.wait_ge(piece_loaded[k], (g + 1) * (16 * PIECE_DMAS))
                        for half in range(2):
                            dve.wait_ge(xq_loaded[half], (g + 1) * 16)
                        turn_rows(g + 1)
                    if load_next and c == LOAD_C and s == AT_XLO:
                        x_low(g + 1)

            nc.vector.memset(ws[:, 4, :], 0.0).then_inc(ws_zero, 1)
            dve.wait_ge(setup_w, 16 * 8)
            dve.wait_ge(ws_zero, 1)
            nc.vector.tensor_copy(ws[:, 0, 0:128:4], w0s[:, 0:1024:33])
            for s in range(1, 16):
                n = F - s
                dst = ws[:, s // 4, s % 4:128:4]
                nc.vector.tensor_tensor(dst[:, 0:n], w0s[:, s:s + 33 * (n - 1) + 1:33],
                                        w0s[:, 32 * s:32 * s + 33 * (n - 1) + 1:33], ALU.add)
                a, b = 1024 - 32 * s, 32 - s
                nc.vector.tensor_tensor(dst[:, n:32], w0s[:, a:a + 33 * (s - 1) + 1:33],
                                        w0s[:, b:b + 33 * (s - 1) + 1:33], ALU.add)
            for r in range(2):
                last = nc.vector.tensor_tensor(ws[:, 4, 64 * r:64 * r + 64:4], w0s[:, 16:16 + 33 * 15 + 1:33],
                                               w0s[:, 512:512 + 33 * 15 + 1:33], ALU.add)
            last.then_inc(ws_laid, 1)
            nc.vector.tensor_copy(w1p.rearrange("p (m h) -> p m h", h=H),
                                  w1s.rearrange("p (h m) -> p m h", m=F)).then_inc(w1_laid, 1)
            nc.vector.tensor_copy(Sel[:, :, :].rearrange("p k n -> p (k n)"), selF).then_inc(sel_ready, 1)
            nc.vector.memset(W2p[:, :, :, :].bitcast(F32), 0.0).then_inc(w_lo, 1)
            dve.wait_ge(w_lo, 1)
            for bq in range(4):
                last = nc.vector.tensor_copy(W2p[:, 0, bq, 32 * bq:32 * bq + 32], w2f[:, :])
            last.then_inc(w_lo, 1)
            dve.wait_ge(w_lo, 2)
            for bq in range(4):
                cols = slice(32 * bq, 32 * bq + 32)
                last = nc.vector.tensor_tensor(W2p[:, 1, bq, cols], w2f[:, :], W2p[:, 0, bq, cols].bitcast(F32),
                                               ALU.subtract)
            last.then_inc(w_lo, 1)
            turn_rows(0)
            dve.wait_ge(w_hi, 4)
            nc.vector.tensor_tensor(Wlo[:, 0:4, :], pz0[:, :].rearrange("p (k n) -> p k n", n=128),
                                    Whi[:, 0:4, :].bitcast(F32), ALU.subtract)
            nc.vector.tensor_tensor(Wlo[:, 4, :], pV[:, 0:128], Whi[:, 4, :].bitcast(F32), ALU.subtract)
            nc.vector.tensor_tensor(Wlo[:, 5:N_TILES, :], pB[:, :, :, :].rearrange("p a t (k n) -> p (a t k) n", n=128),
                                    Whi[:, 5:N_TILES, :].bitcast(F32), ALU.subtract).then_inc(w_lo, 1)
            x_low(0)

            for x in prologue_slots():
                product(x)
                low_part(x)
            for c in range(CH):
                chunk(0, c, True)
            with dve.Fori(1, G - 1) as i:
                for c in range(CH):
                    chunk(i, c, True)
            for c in range(CH):
                chunk(G - 1, c, False, last=c == CH - 1)
            for x in slots_of(G - 1, CH - 1, True)[-LOW_BACK:]:
                low_part(x)
            h1_low(NQ)
            direct_sum(G - 1, CH - 1, NQ)
            dve.wait_ge(direct_used, NQ)
            nc.vector.memset(aux, 0.0).then_inc(zeroed, 1)
            z2_product(G - 1, 1, NQ)
            z2_turn(2 * G)
            z2_reduce(2 * G)

        @block.scalar
        def _(act):
            def high_part(x):
                if not x.split:
                    return
                if x.maker == "v":
                    act.wait_ge(made_v, x.made_v)
                else:
                    act.wait_ge(made_g, x.made_g)
                if x.kind == "L0x":
                    nc.scalar.copy(Pxparts[:, :], P[:, x.p, 0, :]).then_inc(hi_ready, 1)
                    return
                if x.part_free is not None:
                    act.wait_ge(main_done, x.part_free)
                made = P if x.maker == "v" else Pg
                nc.scalar.copy(Phi[:, x.part, :, :], made[:, x.p, :, :]).then_inc(hi_ready, 1)

            def x_high(g):
                act.wait_ge(x_ready, g + 1)
                nc.scalar.copy(Xparts[:, 0, :], X[:, :]).then_inc(xhi_ready, 1)

            def load_piece(c):
                part = slice(32 * (c % 4), 32 * (c % 4) + 32)
                cols = slice(T * (c // 4), T * (c // 4) + T)
                act.dma_start(S[0:64, c, :].bitcast(F32),
                              Xparts[part, :, cols].bitcast(F32)).then_inc(piece_loaded[c], 16)
                act.dma_start(xrep[:, c, :], X[part, cols].unsqueeze(1)
                              .broadcast_to([32, 4, T])).then_inc(piece_loaded[c], 16)

            def load_xq(half):
                act.dma_start(XQ[:, half, :], X[:, half * T:half * T + T]).then_inc(xq_loaded[half], 16)

            def chunk_is_made(q):
                act.wait_ge(made_v, q * MADE_V + N0)
                act.wait_ge(made_g, q * MADE_G)

            def z1_out(c, q, main):
                act.wait_ge(main_done, main)
                if not isinstance(q, int) or q > 1:
                    act.wait_ge(v_done, q - 1)
                z = pz1[:, c % 2, :]
                nc.scalar.activation(h1[0:H, :], z[0:H, :], ACT.Relu, bias=b1t[0:H, :])
                nc.scalar.activation(h1f[:, :], z[0:H, :], ACT.Relu, bias=b1t[0:H, :]).then_inc(h1_ready, 1)
                nc.scalar.activation(direct[H:128, c % 2, :], z[H:128, :], ACT.Relu,
                                     bias=b1t[H:128, :]).then_inc(z1_read, 1)

            def z0_out(c, main, used):
                act.wait_ge(main_done, main)
                nc.scalar.activation(hdup[0:H, c % 2, :], pz0[0:H, :], ACT.Relu, bias=b0t[0:H, :])
                nc.scalar.activation(hdup[H:128, c % 2, :], pz0[0:H, :], ACT.Relu,
                                     bias=b0t[0:H, :]).then_inc(h0_ready, 1)
                if used is not None:
                    act.wait_ge(direct_used, used)
                nc.scalar.activation(direct[0:H, c % 2, :], pz0[H:128, :], ACT.Relu,
                                     bias=b0t[H:128, :]).then_inc(z0_read, 1)

            def chunk(g, c, load_next, last=False):
                q = CH * g + c
                first = isinstance(g, int) and g == 0 and c == 0
                loaded = not (isinstance(g, int) and g == 0)
                for s, x in enumerate(slots_of(g, c, last)):
                    high_part(x)
                    if s == AT_Z1 and not first:
                        z1_out((c - 1) % CH, q, q * NS + N0)
                    if s == AT_Z0 and not last:
                        if not first:
                            chunk_is_made(q)
                        z0_out((c + 1) % CH, q * NS + (N0 + L0X_AT + 1), None if first else q)
                    if load_next and c == LOAD_C and s == AT_XHI:
                        x_high(g + 1)
                    piece = LOAD_AT.get((c, s)) if (load_next if c >= LOAD_C else loaded) else None
                    half = LOAD_XQ_AT.get((c, s)) if (load_next if c >= LOAD_C else loaded) else None
                    if piece == 0:
                        act.wait_ge(xlo_ready, g + 2)
                    if piece in (0, 6, 7):
                        chunk_is_made(q)
                    if piece is not None:
                        load_piece(piece)
                    if half is not None:
                        act.wait_ge(q_done, g * 2 + 1 - half)
                        load_xq(half)

            x_high(0)
            act.wait_ge(w_turned, 3)
            turned = [(slice(0, 4), pz0[:, :].rearrange("p (k n) -> p k n", n=128)),
                      (slice(4, 5), pV[:, 0:128].rearrange("p (k n) -> p k n", n=128)),
                      (slice(5, 13), pB[:, 0, :, :].rearrange("p t (k n) -> p (t k) n", n=128)),
                      (slice(13, 21), pB[:, 1, :, :].rearrange("p t (k n) -> p (t k) n", n=128))]
            for k, psum in turned:
                for n, tile in enumerate(WHOLE_TILES):
                    if k.start <= tile < k.stop:
                        nc.scalar.copy(Wf[:, n, :], psum[:, tile - k.start, :])
                nc.scalar.copy(Whi[:, k, :], psum).then_inc(w_hi, 1)

            act.wait_ge(xlo_ready, 1)
            act.wait_ge(ws_laid, 1)
            act.wait_ge(sel_ready, 1)
            for c in range(CH):
                load_piece(c)
                if c == 3:
                    load_xq(0)
            load_xq(1)
            for x in prologue_slots():
                high_part(x)
            z0_out(0, N0, None)
            for c in range(CH):
                chunk(0, c, True)
            with act.Fori(1, G - 1) as i:
                for c in range(CH):
                    chunk(i, c, True)
            for c in range(CH):
                chunk(G - 1, c, False, last=c == CH - 1)
            z1_out(CH - 1, NQ, slots_of(G - 1, CH - 1, True)[-1].done)

            act.wait_ge(setup_c, 16 * 16)
            act.wait_ge(zeroed, 3)
            act.wait_ge(dense_turned, 1)
            nc.scalar.copy(aux[0:DENSE, :, :].rearrange("p q (g r) -> p q g r", r=32),
                           pB[0:DENSE, :, :, :].rearrange("p a t (g q r) -> p q (a t g) r", q=4, r=32))
            act.wait_ge(z2_sum, 2 * G)
            nc.scalar.activation(z2r[:, :], z2s[:, :, :].rearrange("p g b -> p (g b)"), ACT.Relu,
                                 bias=b2t[:, :]).then_inc(z2_relu, 1)
            act.wait_ge(z2_row, 1)
            nc.scalar.copy(aux[32:36, :, :], pV[0:4, :].unsqueeze(1).broadcast_to([4, 4, T])).then_inc(aux_ready, 1)

            def hid1_out(bq):
                for m in range(4):
                    act.wait_ge(hid1_done, 4 * bq + m + 1)
                    if bq >= 2 and m == 0:
                        act.wait_ge(hid2_done, 2 * (bq - 1))
                    nc.scalar.activation(hid1[:, bq % 2, m, :], pB[:, m // 2, m % 2, :], ACT.Relu,
                                         bias=bt1[:, m:m + 1]).then_inc(hid1_act, 1)

            def hid2_out(bq):
                for m in range(2):
                    act.wait_ge(hid2_done, 2 * bq + m + 1)
                    if bq >= 2 and m == 0:
                        act.wait_ge(y_done, bq - 1)
                    nc.scalar.activation(hid2[:, bq % 2, m, :], pz1[:, m, :], ACT.Relu,
                                         bias=bt2[:, m:m + 1]).then_inc(hid2_act, 1)

            hid1_out(0)
            for bq in range(4):
                if bq < 3:
                    hid1_out(bq + 1)
                hid2_out(bq)
                act.wait_ge(y_done, bq + 1)
                nc.scalar.copy(y[0:1, bq, :], pz0[0:1, :]).then_inc(y_copied, 1)

        @block.tensor
        def _(pe):
            def broadcast(x):
                if x.maker != "v":
                    return
                if not isinstance(x.made_v, int) or x.made_v > 2:
                    pe.wait_ge(made_v, x.made_v - 2)
                if x.kind == "L0" and x.tile == 0:
                    pe.wait_ge(piece_loaded[x.piece], (x.group + 1) * (16 * PIECE_DMAS))
                first, n = {"L0": (2 * x.tile, 2), "L0x": (4, 1), "L1": (5 + 2 * x.tile, 2)}[x.kind]
                for t in range(n):
                    last = nc.tensor.matmul(pB[:, x.bank, t, :], Sel[:, SEL_TILES.index(first + t), :], S[:, x.piece, :],
                                            start=True, stop=True)
                last.then_inc(bcast_ready, 1)

            def main(x):
                if x.split:
                    pe.wait_ge(lo_ready, x.parts)
                else:
                    pe.wait_ge(made_g, x.made_g)
                if x.kind == "L0x":
                    nc.tensor.matmul(pz0[:, :], Wlo[:, 4, :], Pxparts[:, :], start=False, stop=False)
                    last = nc.tensor.matmul(pz0[:, :], Whi[:, 4, :], Pxparts[:, :], start=False, stop=True)
                    last.then_inc(main_done, 1)
                    return
                if x.kind == "L0":
                    acc, first, opens, closes = pz0[:, :], 2 * x.tile, x.tile == 0, False
                    if opens and not (isinstance(x.q, int) and x.q == 0):
                        pe.wait_ge(z0_read, x.q)
                else:
                    acc, first, opens, closes = pz1[:, x.piece % 2, :], 5 + 2 * x.tile, x.tile == 0, x.tile == 7
                    if opens and not (isinstance(x.q, int) and x.q < 2):
                        pe.wait_ge(z1_read, x.q - 1)
                for t in range(2):
                    if x.split:
                        hi, lo = Phi[:, x.part, t, :], Plo[:, x.part, t, :]
                        nc.tensor.matmul(acc, Wlo[:, first + t, :], hi, start=opens and t == 0, stop=False)
                        nc.tensor.matmul(acc, Whi[:, first + t, :], hi, start=False, stop=False)
                        last = nc.tensor.matmul(acc, Whi[:, first + t, :], lo, start=False, stop=closes and t == 1)
                    else:
                        last = nc.tensor.matmul(acc, Wf[:, WHOLE_TILES.index(first + t), :], Pg[:, x.p, t, :],
                                                start=opens and t == 0, stop=closes and t == 1)
                last.then_inc(main_done, 1)

            def layer2(g, c, q):
                pe.wait_ge(h1lo_ready, q)
                if c % 4 == 0 and not (isinstance(g, int) and g == 0 and c == 0):
                    pe.wait_ge(q_done, 2 * g + c // 4)
                nc.tensor.matmul(pV[:, :], W2p[:, 1, c % 4, :], h1[:, :], start=c % 4 == 0, stop=False)
                nc.tensor.matmul(pV[:, :], W2p[:, 0, c % 4, :], h1[:, :], start=False,
                                 stop=c % 4 == 3).then_inc(v_done, 1)

            def chunk(g, c, last=False):
                q = CH * g + c
                slots = slots_of(g, c, last)
                first = isinstance(g, int) and g == 0 and c == 0
                for s, x in enumerate(slots):
                    broadcast(x)
                    behind = back(g, c, s, LAG, slots)
                    if behind is not None:
                        main(behind)
                    if s == min(AT_V, len(slots) - 1) and not first:
                        layer2(g if c else g - 1, (c - 1) % CH, q)

            pe.wait_ge(setup_w, 16 * 8)
            pe.wait_ge(ws_laid, 1)
            for k in range(L0_TILES):
                last = nc.tensor.transpose(pz0[:, 128 * k:128 * k + 128], ws[:, k, :], ident[:, :])
            last.then_inc(w_turned, 1)
            nc.tensor.transpose(pV[:, 0:128], ws[:, 4, :], ident[:, :]).then_inc(w_turned, 1)
            pe.wait_ge(w1_laid, 1)
            for k in range(L1_TILES):
                last = nc.tensor.transpose(pB[:, k // 8, (k // 4) % 2, 128 * (k % 4):128 * (k % 4) + 128],
                                           w1p[:, 128 * k:128 * k + 128], ident[:, :])
            last.then_inc(w_turned, 1)
            pe.wait_ge(w_lo, 4)
            pe.wait_ge(sel_ready, 1)
            pe.wait_ge(zeroed, 1)

            for x in prologue_slots():
                broadcast(x)
            for x in prologue_slots():
                main(x)
            for c in range(CH):
                chunk(0, c)
            with pe.Fori(1, G - 1) as i:
                for c in range(CH):
                    chunk(i, c)
            for c in range(CH):
                chunk(G - 1, c, last=c == CH - 1)
            for x in slots_of(G - 1, CH - 1, True)[-LAG:]:
                main(x)

            pe.wait_ge(made_v, slots_of(G - 1, CH - 1, True)[-1].made_v)
            pe.wait_ge(setup_c, 16 * 16)
            for g in range(G):
                last = nc.tensor.transpose(pB[0:DENSE, g // 8, (g // 4) % 2, 128 * (g % 4):128 * (g % 4) + 128],
                                           dense[:, g, :], ident[:, :])
            last.then_inc(dense_turned, 1)
            layer2(G - 1, CH - 1, NQ)
            pe.wait_ge(z2_relu, 1)
            nc.tensor.matmul(pV[0:4, :], ones4[:, :], z2r[:, :], start=True, stop=True).then_inc(z2_row, 1)
            pe.wait_ge(aux_ready, 1)
            pe.wait_ge(direct_used, NQ)

            def to_hid1(bq):
                for m in range(4):
                    cols = slice(128 * m, 128 * m + 128)
                    bank = pB[:, m // 2, m % 2, :]
                    if bq >= 1:
                        pe.wait_ge(hid1_act, 4 * (bq - 1) + m + 1)
                    nc.tensor.matmul(bank, wt1[:, cols], feat[:, bq, :], start=True, stop=False)
                    nc.tensor.matmul(bank, wta[:, bq, cols], aux[:, bq, :], start=False,
                                     stop=True).then_inc(hid1_done, 1)

            def to_hid2(bq):
                for m in range(2):
                    if m == 0:
                        pe.wait_ge(hid1_act, 4 * bq + 4)
                    if bq >= 1:
                        pe.wait_ge(hid2_act, 2 * (bq - 1) + m + 1)
                    for k in range(4):
                        last = nc.tensor.matmul(pz1[:, m, :], wt2[:, k, 128 * m:128 * m + 128],
                                                hid1[:, bq % 2, k, :], start=k == 0, stop=k == 3)
                    last.then_inc(hid2_done, 1)

            def to_y(bq):
                pe.wait_ge(hid2_act, 2 * bq + 2)
                if bq >= 1:
                    pe.wait_ge(y_copied, bq)
                for k in range(2):
                    last = nc.tensor.matmul(pz0[0:1, :], wt3[:, k, :], hid2[:, bq % 2, k, :],
                                            start=k == 0, stop=k == 1)
                last.then_inc(y_done, 1)

            to_hid1(0)
            for bq in range(4):
                if bq < 3:
                    to_hid1(bq + 1)
                to_hid2(bq)
                to_y(bq)


_FLOATS = ["dense_ctx", "ids", "W_top1", "b_top1", "W_top2", "b_top2", "W_top3",
           "L0_rec_W0", "L0_rec_b0", "L0_rec_W1", "L0_rec_b1", "L0_rec_W2", "L0_rec_b2"]


def _constants():
    import numpy as np

    sel = np.zeros((128, N_TILES, 128), np.float32)
    for part in (0, 1):
        for j in range(128):
            i, shift = j // 4, j % 4
            for t in range(L0_TILES):
                sel[2 * ((i + 4 * t + shift) % 32) + part, t, j] = 1
            sel[2 * ((i + 16) % 32) + part, L0_TILES, j] = 1
            for k in range(L1_TILES):
                sel[2 * (2 * k + j // 64) + part, L0_TILES + 1 + k, j] = 1
    ones = np.zeros((128, 4), np.float32)
    for q in range(4):
        ones[32 * q:32 * q + 32, q] = 1
    return {"sel": sel[:, SEL_TILES, :].reshape(128, -1), "ident": np.eye(128, dtype=np.float32), "ones": ones}


def kernel(**inputs):
    import numpy as np
    import concourse.bacc as bacc
    from concourse.bass_utils import run_bass_kernel_spmd

    nc = bacc.Bacc("TRN2", target_bir_lowering=False, num_devices=1)
    arrays = {}

    def dram(name, a):
        arrays[name] = np.ascontiguousarray(a)
        return nc.dram_tensor(name, a.shape, mybir.dt.from_np(a.dtype), kind="ExternalInput").ap()

    tables = [dram(f"tbl_{f}", np.asarray(inputs[f"tbl_{f}"])) for f in range(F)]
    args = [dram("in_" + n, np.asarray(inputs[n])) for n in _FLOATS]
    consts = [dram("c_" + n, a) for n, a in _constants().items()]
    out = nc.dram_tensor("y_out", (B, 1), F32, kind="ExternalOutput").ap()
    build(nc, tables, *args, *consts, out)
    r = run_bass_kernel_spmd(nc, [arrays], core_ids=[0])
    return r.results[0]["y_out"]
```

```python
import concourse.bass as bass
from concourse import mybir
from contextlib import ExitStack

F32 = mybir.dt.float32
F32R = mybir.dt.float32r
I32 = mybir.dt.int32
ALU = mybir.AluOpType
ACT = mybir.ActivationFunctionType
AX = mybir.AxisListType

B, F, D = 2048, 32, 32
O = 128
H = O // 2
DENSE, HID1 = 16, 512
G = B // 128
CH = 8
T = 512
SB = T // D
NQ = G * CH
L0_TILES = 4
L1_TILES = 16
N_TILES = L0_TILES + 1 + L1_TILES
LAG = 5
LOW_BACK = 2
P_RING, PG_RING, PART_RING, BX_RING = 3, 4, 4, 2
PIECE_DMAS = 2

L0_STREAM = [("L0", 0, "v", "pe", True), ("L0", 1, "v", "pe", True), ("L0x", 0, "v", "pe", True)]
STREAM = [("L0", 0, "v", "pe", True), ("L1", 0, "g", "dma", False), ("L0", 1, "v", "pe", True),
          ("L1", 1, "g", "dma", True), ("L0x", 0, "v", "pe", True), ("L1", 2, "g", "dma", False),
          ("L1", 3, "v", "pe", True), ("L1", 4, "g", "dma", True), ("L1", 5, "v", "dma", True),
          ("L1", 6, "g", "dma", False), ("L1", 7, "v", "pe", True)]
LAST_STREAM = [k for k in STREAM if k[0] == "L1"]
WHOLE_TILES = [L0_TILES + 1 + 2 * k[1] + t for k in STREAM if not k[4] for t in range(2)]
SEL_TILES = list(range(L0_TILES + 1)) + [L0_TILES + 1 + 2 * k[1] + t for k in STREAM
                                         if k[0] == "L1" and k[3] == "pe" for t in range(2)]
NS, N0 = len(STREAM), len(L0_STREAM)
L0X_AT = STREAM.index(L0_STREAM[-1])
AT_Z1 = LAG - 1
AT_Z0 = L0X_AT + LAG
AT_H1LO = 6
AT_DIRECT = 7
AT_V = 8
AT_Q = 9
GATHER_S, GATHER_STEP = 3, 2
FIRST_PIECES = 2
HEAD_C = 3
LOAD_C = 6
AT_X = 1
AT_XHI = 2
AT_XLO = 4
LOAD_AT = {(6, 6): 0, (6, 8): 1, (6, 10): 2, (7, 1): 3, (7, 3): 4, (7, 5): 5, (7, 7): 6, (0, 2): 7}
LOAD_XQ_AT = {(7, 9): 0, (1, 1): 1}


def is_made(by):
    return lambda k: k[2] == by


def is_spread(by, engine):
    return lambda k: (k[3], k[2]) == (by, engine)


def is_split(k):
    return k[4]


def is_pair(k):
    return k[4] and k[0] != "L0x"


class Slot:

    def __init__(self, g, c, s, stream, prologue=False):
        self.kind, self.tile, self.maker, self.spread, self.split = stream[s]
        before = L0_STREAM[:s + 1] if prologue else L0_STREAM + STREAM * c + stream[:s + 1]

        def count(which):
            return sum(map(which, before))

        def over_groups(which):
            return count(which) if prologue else g * sum(map(which, STREAM * CH)) + count(which)

        def before_in_ring(which, ring, of=bool):
            known = before if isinstance(g, int) and g == 0 else STREAM * 2 + before[N0:]
            at = [i for i, k in enumerate(known) if which(k)]
            if len(at) <= ring:
                return None
            return over_groups(of) - sum(map(of, known[at[-1 - ring] + 1:at[-1] + 1]))

        self.done = over_groups(bool)
        self.made_v, self.made_g = over_groups(is_made("v")), over_groups(is_made("g"))
        self.parts = over_groups(is_split)
        ring = P_RING if self.maker == "v" else PG_RING
        self.p = (count(is_made(self.maker)) - 1) % ring
        self.p_free = before_in_ring(is_made(self.maker), ring, is_split if self.maker == "v" else bool)
        if self.spread == "pe":
            self.bcast = over_groups(is_spread("pe", "v"))
            self.bank = (count(is_spread("pe", "v")) - 1) % 2
            self.bank_free = before_in_ring(is_spread("pe", "v"), 2, is_made("v"))
        else:
            mine = is_spread("dma", self.maker)
            n = count(mine)
            self.bx = (n - 1) % BX_RING
            self.bx_uses = g * (sum(map(mine, STREAM * CH)) // BX_RING) + (n - 1) // BX_RING + 1
            self.bx_free = before_in_ring(mine, BX_RING, is_made(self.maker))
        if is_pair(stream[s]):
            self.part = (count(is_pair) - 1) % PART_RING
            self.part_free = before_in_ring(is_pair, PART_RING)
        q = CH * g + c
        if self.kind == "L1":
            self.piece, self.q = c, q
        elif prologue:
            self.piece, self.q, self.group = 0, 0, 0
        else:
            self.piece, self.q = (c + 1) % CH, q + 1
            self.group = g + (c + 1) // CH


assert all(sum(map(which, STREAM)) * CH % ring == 0
           for which, ring in ((is_made("v"), P_RING), (is_spread("pe", "v"), 2), (is_made("g"), PG_RING),
                               (is_spread("dma", "v"), BX_RING), (is_spread("dma", "g"), BX_RING),
                               (is_pair, PART_RING)))
assert all(k[4] if k[2] == "v" else k[3] == "dma" for k in STREAM)
assert all(k[0] == "L1" for k in STREAM if k[3] == "dma")
MADE_V, MADE_G = sum(map(is_made("v"), STREAM)), sum(map(is_made("g"), STREAM))


def slots_of(g, c, last=False):
    stream = LAST_STREAM if last else STREAM
    return [Slot(g, c, s, stream) for s in range(len(stream))]


def prologue_slots():
    return [Slot(0, 0, s, L0_STREAM, prologue=True) for s in range(N0)]


def back(g, c, s, k, slots):
    if s >= k:
        return slots[s - k]
    if c == 0 and isinstance(g, int) and g == 0:
        return None
    return slots_of(g - 1 if c == 0 else g, (c - 1) % CH)[s - k]


def build(nc, tables, dense_ctx, ids, W_top1, b_top1, W_top2, b_top2, W_top3, W0, b0, W1, b1, W2, b2,
          sel_c, ident_c, ones_c, out):
    ctx = ExitStack()
    with ctx:
        def sb(name, shape, dt=F32):
            return ctx.enter_context(nc.sbuf_tensor(name, shape, dt))

        def ps(name, shape):
            return ctx.enter_context(nc.psum_tensor(name, shape, F32))

        def sem(name):
            return ctx.enter_context(nc.semaphore(name))

        idx = sb("idx", [128, F], I32)
        rows = sb("rows", [128, F * D])
        X = sb("X", [128, 2 * T])
        Xparts = sb("Xparts", [128, 2, 2 * T], F32R)
        S = sb("S", [128, CH, T], F32R)
        xrep = sb("xrep", [128, CH, T])
        XQ = sb("XQ", [128, 2, T])
        BX = {"g": sb("BXg", [128, BX_RING, 2, T]), "v": sb("BXv", [128, BX_RING, 2, T])}
        P = sb("P", [128, P_RING, 2, T])
        Pg = sb("Pg", [128, PG_RING, 2, T])
        Phi = sb("Phi", [128, PART_RING, 2, T], F32R)
        Plo = sb("Plo", [128, PART_RING, 2, T], F32R)
        Pxparts = sb("Pxparts", [128, T], F32R)
        hdup = sb("hdup", [128, 2, T])
        direct = sb("direct", [128, 2, T])
        h1f = sb("h1f", [H, T])
        h1 = sb("h1", [128, T], F32R)
        Qp = sb("Qp", [128, T])
        Qt = sb("Qt", [128, T])
        z2s = sb("z2s", [128, G * 2, SB])
        feat = sb("feat", [128, 4, G * 2 * SB])
        Sel = sb("Sel", [128, len(SEL_TILES), 128], F32R)
        Whi = sb("Whi", [128, N_TILES, 128], F32R)
        Wlo = sb("Wlo", [128, N_TILES, 128], F32R)
        Wf = sb("Wf", [128, len(WHOLE_TILES), 128])
        w2f = sb("w2f", [128, F])
        W2p = sb("W2p", [128, 2, 4, 128], F32R)
        ident = sb("ident", [128, 128])
        ones4 = sb("ones4", [128, 4])
        b0t, b1t, b2t = sb("b0t", [128, 1]), sb("b1t", [128, 1]), sb("b2t", [128, 1])
        bt1, bt2 = sb("bt1", [128, 4]), sb("bt2", [128, 2])
        wt1 = X[:, 0:HID1]
        wt2 = rows[:, :].rearrange("p (k n) -> p k n", k=4)
        wta = Xparts[0:36, :, :].bitcast(F32).rearrange("p a (e n) -> p (a e) n", n=HID1)
        wt3 = sb("wt3", [128, 2, 1])
        dense = sb("dense", [128, G, DENSE])
        aux = sb("aux", [36, 4, T])
        w1s = Pg[:, 0:2, :, :].rearrange("p r t n -> p (r t n)")
        w1p = Pg[:, 2:4, :, :].rearrange("p r t n -> p (r t n)")
        flat = xrep[:, :, :].rearrange("p c n -> p (c n)")
        selF = flat[:, 0:len(SEL_TILES) * 128]
        w0s = flat[:, 3072:4096]
        ws = P[:, 0, :, :].rearrange("p t n -> p (t n)")[:, 0:5 * 128].rearrange("p (k n) -> p k n", k=5)
        z2r = Qt
        hid1 = Pg[:, :, :, :].rearrange("p (e r) t n -> p e (r t) n", e=2)
        hid2 = xrep[:, 0:4, :].rearrange("p (e m) n -> p e m n", e=2)
        y = xrep[0:1, 4:8, :]

        pB = ps("pB", [128, 2, 2, T])
        pz0 = ps("pz0", [128, T])
        pz1 = ps("pz1", [128, 2, T])
        pV = ps("pV", [128, T])

        setup_w = sem("setup_w")
        setup_c = sem("setup_c")
        idx_loaded = sem("idx_loaded")
        gathered = sem("gathered")
        zeroed = sem("zeroed")
        w1_laid = sem("w1_laid")
        ws_zero = sem("ws_zero")
        ws_laid = sem("ws_laid")
        w_turned = sem("w_turned")
        w_hi = sem("w_hi")
        w_lo = sem("w_lo")
        sel_ready = sem("sel_ready")
        x_ready = sem("x_ready")
        xhi_ready = sem("xhi_ready")
        xlo_ready = sem("xlo_ready")
        piece_loaded = [sem(f"piece_loaded{c}") for c in range(CH)]
        xq_loaded = [sem(f"xq_loaded{h}") for h in range(2)]
        bcast_ready = sem("bcast_ready")
        made_v = sem("made_v")
        made_g = sem("made_g")
        bx_loaded = {e: [sem(f"bx{e}_loaded{r}") for r in range(BX_RING)] for e in "gv"}
        hi_ready = sem("hi_ready")
        lo_ready = sem("lo_ready")
        main_done = sem("main_done")
        h0_ready = sem("h0_ready")
        z0_read = sem("z0_read")
        h1_ready = sem("h1_ready")
        h1lo_ready = sem("h1lo_ready")
        z1_read = sem("z1_read")
        direct_used = sem("direct_used")
        v_done = sem("v_done")
        q_done = sem("q_done")
        qt_done = sem("qt_done")
        z2_sum = sem("z2_sum")
        z2_relu = sem("z2_relu")
        z2_row = sem("z2_row")
        dense_turned = sem("dense_turned")
        aux_zero = sem("aux_zero")
        dense_ready = sem("dense_ready")
        aux_ready = sem("aux_ready")
        hid1_done, hid1_act = sem("hid1_done"), sem("hid1_act")
        hid2_done, hid2_act = sem("hid2_done"), sem("hid2_act")
        y_done, y_copied, stored = sem("y_done"), sem("y_copied"), sem("stored")

        ids_g = ids.rearrange("(g p) f -> g p f", p=128)
        block = ctx.enter_context(nc.Block())

        @block.sync
        def _(sp):
            def load_idx(g):
                sp.dma_start(idx[:, :], ids_g[g]).then_inc(idx_loaded, 16)

            def chunk(g, c, load_next, last=False):
                for x in [x for x in slots_of(g, c, last) if x.spread == "dma"]:
                    if x.bx_free is not None:
                        sp.wait_ge(made_g if x.maker == "g" else made_v, x.bx_free)
                    if x.tile == 0:
                        if load_next and c == 0:
                            sp.wait_ge(gathered, (g + 1) * (16 * F))
                            load_idx(g + 1)
                        sp.wait_ge(piece_loaded[c], (g + 1) * (16 * PIECE_DMAS))
                    for t in range(2):
                        k = 2 * x.tile + t
                        sp.dma_start(BX[x.maker][:, x.bx, t, :], xrep[8 * k:8 * k + 8, c, :].unsqueeze(1)
                                     .broadcast_to([8, 16, T])).then_inc(bx_loaded[x.maker][x.bx], 16)

            def load_first(c):
                if c + FIRST_PIECES < CH:
                    piece = c + FIRST_PIECES
                    part = slice(32 * (piece % 4), 32 * (piece % 4) + 32)
                    cols = slice(T * (piece // 4), T * (piece // 4) + T)
                    sp.dma_start(S[0:64, piece, :].bitcast(F32),
                                 Xparts[part, :, cols].bitcast(F32)).then_inc(piece_loaded[piece], 16)
                    sp.dma_start(xrep[:, piece, :], X[part, cols].unsqueeze(1)
                                 .broadcast_to([32, 4, T])).then_inc(piece_loaded[piece], 16)
                if c < 2:
                    sp.dma_start(XQ[:, c, :], X[:, c * T:c * T + T]).then_inc(xq_loaded[c], 16)

            load_idx(0)
            sp.dma_start(w0s, W0).then_inc(setup_w, 16)
            sp.dma_start(ident[:, :], ident_c).then_inc(setup_w, 16)
            sp.dma_start(w1s, W1).then_inc(setup_w, 16)
            sp.dma_start(w2f[0:H, :], W2.rearrange("o (h m) -> (o h) m", m=F)).then_inc(setup_w, 16)
            sp.dma_start(w2f[H:128, :], W2.rearrange("o (h m) -> (o h) m", m=F)).then_inc(setup_w, 16)
            sp.dma_start(selF, sel_c).then_inc(setup_w, 16)
            sp.dma_start(b0t[:, :], b0.rearrange("(p o) -> p o", o=1)).then_inc(setup_w, 16)
            sp.dma_start(b1t[:, :], b1.rearrange("(p o) -> p o", o=1)).then_inc(setup_w, 16)
            sp.dma_start(dense[:, :, :], dense_ctx.rearrange("(g p) c -> p g c", p=128)).then_inc(setup_w, 16)
            sp.dma_start(ones4[:, :], ones_c).then_inc(setup_c, 16)
            sp.dma_start(b2t[:, :], b2.rearrange("(p o) -> p o", o=1).broadcast_to([128, 1])).then_inc(setup_c, 16)
            sp.dma_start(bt1[:, :], b_top1.rearrange("(m p) -> p m", p=128),
                         allow_slow_non_contiguous=True).then_inc(setup_c, 16)
            sp.dma_start(bt2[:, :], b_top2.rearrange("(m p) -> p m", p=128),
                         allow_slow_non_contiguous=True).then_inc(setup_c, 16)
            sp.dma_start(wt3[:, :, :], W_top3.rearrange("(k p) n -> p k n", p=128),
                         allow_slow_non_contiguous=True).then_inc(setup_c, 16)

            sp.wait_ge(ws_laid, 1)
            sp.wait_ge(sel_ready, 1)
            sp.wait_ge(xlo_ready, 1)
            for c in range(FIRST_PIECES):
                sp.wait_ge(piece_loaded[c], 16 * PIECE_DMAS)
            for c in range(CH):
                load_first(c)
                chunk(0, c, True)
            with sp.Fori(1, G - 1) as i:
                for c in range(CH):
                    chunk(i, c, True)
            for c in range(CH):
                if c == HEAD_C:
                    sp.wait_ge(zeroed, 2)
                    sp.dma_start(wt1[:, :], W_top1[0:128, :]).then_inc(setup_c, 16)
                    sp.dma_start(wt2[:, :, :], W_top2.rearrange("(k p) n -> p k n", p=128)).then_inc(setup_c, 16)
                if c > HEAD_C:
                    bq = c - HEAD_C - 1
                    sp.dma_start(wta[0:DENSE, bq, :], W_top1[129:145, :]).then_inc(setup_c, 16)
                    sp.dma_start(wta[32 + bq:33 + bq, bq, :], W_top1[128:129, :]).then_inc(setup_c, 16)
                chunk(G - 1, c, False, last=c == CH - 1)

            for bq in range(4):
                sp.wait_ge(y_copied, bq + 1)
                sp.dma_start(out.rearrange("(g q r) o -> q o g r", q=4, r=32)[bq],
                             y[0:1, bq, :].rearrange("p (g r) -> p g r", r=32)).then_inc(stored, 16)
            sp.wait_ge(stored, 64)

        @block.gpsimd
        def _(pool):
            def gather(f):
                nc.gpsimd.indirect_dma_start(
                    rows[:, f * D:(f + 1) * D], None, tables[f],
                    bass.IndirectOffsetOnAxis(ap=idx[:, f:f + 1], axis=0)).then_inc(gathered, 16)

            def product(x):
                if x.maker != "g":
                    return
                if x.tile == 0:
                    pool.wait_ge(h0_ready, x.q + 1)
                if x.p_free is not None:
                    pool.wait_ge(main_done, x.p_free)
                pool.wait_ge(bx_loaded["g"][x.bx], x.bx_uses * 32)
                nc.gpsimd.tensor_tensor(Pg[:, x.p, :, :], BX["g"][:, x.bx, :, :],
                                        hdup[:, x.piece % 2, :].unsqueeze(1).broadcast_to([128, 2, T]),
                                        ALU.mult).then_inc(made_g, 1)

            def chunk(g, c, load_next, last=False):
                for s, x in enumerate(slots_of(g, c, last)):
                    f, off = divmod(c * NS + s - GATHER_S, GATHER_STEP)
                    if load_next and (f, off) == (0, 0):
                        pool.wait_ge(idx_loaded, (g + 2) * 16)
                        pool.wait_ge(x_ready, g + 1)
                    product(x)
                    if load_next and off == 0 and 0 <= f < F:
                        gather(f)

            pool.wait_ge(idx_loaded, 16)
            for f in range(F):
                gather(f)
            nc.gpsimd.memset(S[64:128, :, :].bitcast(F32), 0.0).then_inc(zeroed, 1)
            for c in range(CH):
                chunk(0, c, True)
            with pool.Fori(1, G - 1) as i:
                for c in range(CH):
                    chunk(i, c, True)
            for c in range(CH):
                if c == HEAD_C:
                    for k in range(CH):
                        pool.wait_ge(piece_loaded[k], G * (16 * PIECE_DMAS))
                    for half in range(2):
                        pool.wait_ge(xq_loaded[half], G * 16)
                    nc.gpsimd.memset(wta, 0.0).then_inc(zeroed, 1)
                chunk(G - 1, c, False, last=c == CH - 1)

        @block.vector
        def _(dve):
            def product(x):
                if x.maker != "v":
                    return
                if x.p_free is not None:
                    dve.wait_ge(lo_ready, x.p_free)
                if x.spread == "pe":
                    dve.wait_ge(bcast_ready, x.bcast)
                    factor = pB[:, x.bank, :, :]
                else:
                    dve.wait_ge(bx_loaded["v"][x.bx], x.bx_uses * 32)
                    factor = BX["v"][:, x.bx, :, :]
                if x.kind == "L1":
                    dve.wait_ge(h0_ready, x.q + 1)
                    other = hdup[:, x.piece % 2, :]
                else:
                    dve.wait_ge(piece_loaded[x.piece], (x.group + 1) * (16 * PIECE_DMAS))
                    other = xrep[:, x.piece, :]
                if x.kind == "L0x":
                    nc.vector.tensor_tensor(P[:, x.p, 0, :], factor[:, 0, :], other,
                                            ALU.mult).then_inc(made_v, 1)
                else:
                    nc.vector.tensor_tensor(P[:, x.p, :, :], factor,
                                            other.unsqueeze(1).broadcast_to([128, 2, T]),
                                            ALU.mult).then_inc(made_v, 1)

            def low_part(x):
                if x is None or not x.split:
                    return
                dve.wait_ge(hi_ready, x.parts)
                if x.kind == "L0x":
                    part = Pxparts[64:128, :]
                    nc.vector.tensor_tensor(part, P[64:128, x.p, 0, :], part.bitcast(F32),
                                            ALU.subtract).then_inc(lo_ready, 1)
                else:
                    made = P if x.maker == "v" else Pg
                    nc.vector.tensor_tensor(Plo[:, x.part, :, :], made[:, x.p, :, :],
                                            Phi[:, x.part, :, :].bitcast(F32), ALU.subtract).then_inc(lo_ready, 1)

            def h1_low(q):
                dve.wait_ge(h1_ready, q)
                nc.vector.tensor_tensor(h1[H:128, :], h1f[:, :], h1[0:H, :].bitcast(F32),
                                        ALU.subtract).then_inc(h1lo_ready, 1)

            def direct_sum(g, c, q):
                dve.wait_ge(z1_read, q)
                nc.vector.tensor_reduce(
                    feat[:, c % 4, bass.ds(g * 32 + (c // 4) * SB, SB)],
                    direct[:, c % 2, :].rearrange("p (b d) -> p b d", d=D), AX.X, ALU.add).then_inc(direct_used, 1)

            def z2_product(g, half, q):
                dve.wait_ge(v_done, q)
                dve.wait_ge(xq_loaded[half], (g + 1) * 16)
                nc.vector.tensor_tensor(Qp[:, :], pV[:, :], XQ[:, half, :], ALU.mult).then_inc(q_done, 1)

            def z2_turn(n):
                dve.wait_ge(q_done, n)
                nc.vector.transpose(Qt[:, :], Qp[:, :]).then_inc(qt_done, 1)

            def z2_reduce(n):
                dve.wait_ge(qt_done, n)
                nc.vector.tensor_reduce(z2s[:, bass.ds(n - 1, 1), :].rearrange("p o b -> p (o b)"),
                                        Qt[:, :].rearrange("p (b m) -> p b m", m=F), AX.X,
                                        ALU.add).then_inc(z2_sum, 1)

            def turn_rows(g):
                dve.wait_ge(gathered, (g + 1) * (16 * F))
                nc.vector.transpose(X[:, :].rearrange("p (b d) -> p d b", d=D),
                                    rows[:, :].rearrange("p (f d) -> p d f", d=D)).then_inc(x_ready, 1)

            def x_low(g):
                dve.wait_ge(xhi_ready, g + 1)
                nc.vector.tensor_tensor(Xparts[:, 1, :], X[:, :], Xparts[:, 0, :].bitcast(F32),
                                        ALU.subtract).then_inc(xlo_ready, 1)

            def chunk(g, c, load_next, last=False):
                q = CH * g + c
                slots = slots_of(g, c, last)
                first = isinstance(g, int) and g == 0 and c == 0
                for s, x in enumerate(slots):
                    product(x)
                    turn = c % 4 == 0 and not first and s == AT_Q + 1
                    n = 2 * g + c // 4
                    if turn:
                        z2_turn(n)
                    low_part(back(g, c, s, LOW_BACK, slots))
                    if turn:
                        z2_reduce(n)
                    if s == AT_H1LO and not first:
                        h1_low(q)
                    if s == AT_DIRECT and not first:
                        direct_sum(g if c else g - 1, (c - 1) % CH, q)
                    if c % 4 == 0 and not first and s == AT_Q:
                        z2_product(g if c else g - 1, (c // 4 + 1) % 2, q)
                    if load_next and c == LOAD_C and s == AT_X:
                        for k in range(CH):
                            dve.wait_ge(piece_loaded[k], (g + 1) * (16 * PIECE_DMAS))
                        for half in range(2):
                            dve.wait_ge(xq_loaded[half], (g + 1) * 16)
                        turn_rows(g + 1)
                    if load_next and c == LOAD_C and s == AT_XLO:
                        x_low(g + 1)

            nc.vector.memset(ws[:, 4, :], 0.0).then_inc(ws_zero, 1)
            nc.vector.memset(aux[:, :, :], 0.0).then_inc(aux_zero, 1)
            dve.wait_ge(setup_w, 16 * 9)
            dve.wait_ge(ws_zero, 1)
            nc.vector.tensor_copy(ws[:, 0, 0:128:4], w0s[:, 0:1024:33])
            for s in range(1, 16):
                n = F - s
                dst = ws[:, s // 4, s % 4:128:4]
                nc.vector.tensor_tensor(dst[:, 0:n], w0s[:, s:s + 33 * (n - 1) + 1:33],
                                        w0s[:, 32 * s:32 * s + 33 * (n - 1) + 1:33], ALU.add)
                a, b = 1024 - 32 * s, 32 - s
                nc.vector.tensor_tensor(dst[:, n:32], w0s[:, a:a + 33 * (s - 1) + 1:33],
                                        w0s[:, b:b + 33 * (s - 1) + 1:33], ALU.add)
            for r in range(2):
                last = nc.vector.tensor_tensor(ws[:, 4, 64 * r:64 * r + 64:4], w0s[:, 16:16 + 33 * 15 + 1:33],
                                               w0s[:, 512:512 + 33 * 15 + 1:33], ALU.add)
            last.then_inc(ws_laid, 1)
            nc.vector.tensor_copy(w1p.rearrange("p (m h) -> p m h", h=H),
                                  w1s.rearrange("p (h m) -> p m h", m=F)).then_inc(w1_laid, 1)
            nc.vector.tensor_copy(Sel[:, :, :].rearrange("p k n -> p (k n)"), selF).then_inc(sel_ready, 1)
            nc.vector.memset(W2p[:, :, :, :].bitcast(F32), 0.0).then_inc(w_lo, 1)
            dve.wait_ge(w_lo, 1)
            for bq in range(4):
                last = nc.vector.tensor_copy(W2p[:, 0, bq, 32 * bq:32 * bq + 32], w2f[:, :])
            last.then_inc(w_lo, 1)
            dve.wait_ge(w_lo, 2)
            for bq in range(4):
                cols = slice(32 * bq, 32 * bq + 32)
                last = nc.vector.tensor_tensor(W2p[:, 1, bq, cols], w2f[:, :], W2p[:, 0, bq, cols].bitcast(F32),
                                               ALU.subtract)
            last.then_inc(w_lo, 1)
            dve.wait_ge(w_hi, 4)
            nc.vector.tensor_tensor(Wlo[:, 0:4, :], pz0[:, :].rearrange("p (k n) -> p k n", n=128),
                                    Whi[:, 0:4, :].bitcast(F32), ALU.subtract)
            nc.vector.tensor_tensor(Wlo[:, 4, :], pV[:, 0:128], Whi[:, 4, :].bitcast(F32), ALU.subtract)
            nc.vector.tensor_tensor(Wlo[:, 5:N_TILES, :], pB[:, :, :, :].rearrange("p a t (k n) -> p (a t k) n", n=128),
                                    Whi[:, 5:N_TILES, :].bitcast(F32), ALU.subtract).then_inc(w_lo, 1)
            turn_rows(0)
            x_low(0)

            for x in prologue_slots():
                product(x)
                low_part(x)
            for c in range(CH):
                chunk(0, c, True)
            with dve.Fori(1, G - 1) as i:
                for c in range(CH):
                    chunk(i, c, True)
            for c in range(CH):
                chunk(G - 1, c, False, last=c == CH - 1)
            for x in slots_of(G - 1, CH - 1, True)[-LOW_BACK:]:
                low_part(x)
            h1_low(NQ)
            direct_sum(G - 1, CH - 1, NQ)
            z2_product(G - 1, 1, NQ)
            z2_turn(2 * G)
            z2_reduce(2 * G)

        @block.scalar
        def _(act):
            def high_part(x):
                if not x.split:
                    return
                if x.maker == "v":
                    act.wait_ge(made_v, x.made_v)
                else:
                    act.wait_ge(made_g, x.made_g)
                if x.kind == "L0x":
                    nc.scalar.copy(Pxparts[:, :], P[:, x.p, 0, :]).then_inc(hi_ready, 1)
                    return
                if x.part_free is not None:
                    act.wait_ge(main_done, x.part_free)
                made = P if x.maker == "v" else Pg
                nc.scalar.copy(Phi[:, x.part, :, :], made[:, x.p, :, :]).then_inc(hi_ready, 1)

            def x_high(g):
                act.wait_ge(x_ready, g + 1)
                nc.scalar.copy(Xparts[:, 0, :], X[:, :]).then_inc(xhi_ready, 1)

            def load_piece(c):
                part = slice(32 * (c % 4), 32 * (c % 4) + 32)
                cols = slice(T * (c // 4), T * (c // 4) + T)
                act.dma_start(S[0:64, c, :].bitcast(F32),
                              Xparts[part, :, cols].bitcast(F32)).then_inc(piece_loaded[c], 16)
                act.dma_start(xrep[:, c, :], X[part, cols].unsqueeze(1)
                              .broadcast_to([32, 4, T])).then_inc(piece_loaded[c], 16)

            def load_xq(half):
                act.dma_start(XQ[:, half, :], X[:, half * T:half * T + T]).then_inc(xq_loaded[half], 16)

            def chunk_is_made(q):
                act.wait_ge(made_v, q * MADE_V + N0)
                act.wait_ge(made_g, q * MADE_G)

            def z1_out(c, q, main):
                act.wait_ge(main_done, main)
                if not isinstance(q, int) or q > 1:
                    act.wait_ge(v_done, q - 1)
                z = pz1[:, c % 2, :]
                nc.scalar.activation(h1[0:H, :], z[0:H, :], ACT.Relu, bias=b1t[0:H, :])
                nc.scalar.activation(h1f[:, :], z[0:H, :], ACT.Relu, bias=b1t[0:H, :]).then_inc(h1_ready, 1)
                nc.scalar.activation(direct[H:128, c % 2, :], z[H:128, :], ACT.Relu,
                                     bias=b1t[H:128, :]).then_inc(z1_read, 1)

            def z0_out(c, main, used):
                act.wait_ge(main_done, main)
                nc.scalar.activation(hdup[0:H, c % 2, :], pz0[0:H, :], ACT.Relu, bias=b0t[0:H, :])
                nc.scalar.activation(hdup[H:128, c % 2, :], pz0[0:H, :], ACT.Relu,
                                     bias=b0t[0:H, :]).then_inc(h0_ready, 1)
                if used is not None:
                    act.wait_ge(direct_used, used)
                nc.scalar.activation(direct[0:H, c % 2, :], pz0[H:128, :], ACT.Relu,
                                     bias=b0t[H:128, :]).then_inc(z0_read, 1)

            def chunk(g, c, load_next, last=False):
                q = CH * g + c
                first = isinstance(g, int) and g == 0 and c == 0
                loaded = not (isinstance(g, int) and g == 0)
                for s, x in enumerate(slots_of(g, c, last)):
                    high_part(x)
                    if s == AT_Z1 and not first:
                        z1_out((c - 1) % CH, q, q * NS + N0)
                    if s == AT_Z0 and not last:
                        if not first:
                            chunk_is_made(q)
                        z0_out((c + 1) % CH, q * NS + (N0 + L0X_AT + 1), None if first else q)
                    if load_next and c == LOAD_C and s == AT_XHI:
                        x_high(g + 1)
                    piece = LOAD_AT.get((c, s)) if (load_next if c >= LOAD_C else loaded) else None
                    half = LOAD_XQ_AT.get((c, s)) if (load_next if c >= LOAD_C else loaded) else None
                    if piece == 0:
                        act.wait_ge(xlo_ready, g + 2)
                    if piece in (0, 6, 7):
                        chunk_is_made(q)
                    if piece is not None:
                        load_piece(piece)
                    if half is not None:
                        act.wait_ge(q_done, g * 2 + 1 - half)
                        load_xq(half)

            act.wait_ge(w_turned, 3)
            turned = [(slice(0, 4), pz0[:, :].rearrange("p (k n) -> p k n", n=128)),
                      (slice(4, 5), pV[:, 0:128].rearrange("p (k n) -> p k n", n=128)),
                      (slice(5, 13), pB[:, 0, :, :].rearrange("p t (k n) -> p (t k) n", n=128)),
                      (slice(13, 21), pB[:, 1, :, :].rearrange("p t (k n) -> p (t k) n", n=128))]
            for k, psum in turned:
                for n, tile in enumerate(WHOLE_TILES):
                    if k.start <= tile < k.stop:
                        nc.scalar.copy(Wf[:, n, :], psum[:, tile - k.start, :])
                nc.scalar.copy(Whi[:, k, :], psum).then_inc(w_hi, 1)

            act.wait_ge(aux_zero, 1)
            act.wait_ge(dense_turned, 1)
            nc.scalar.copy(aux[0:DENSE, :, :].rearrange("p q (g r) -> p q g r", r=32),
                           pB[0:DENSE, :, :, :].rearrange("p a t (g q r) -> p q (a t g) r", q=4, r=32)
                           ).then_inc(dense_ready, 1)

            x_high(0)
            act.wait_ge(ws_laid, 1)
            act.wait_ge(sel_ready, 1)
            act.wait_ge(xlo_ready, 1)
            for c in range(FIRST_PIECES):
                load_piece(c)
            for x in prologue_slots():
                high_part(x)
            z0_out(0, N0, None)
            for c in range(CH):
                chunk(0, c, True)
            with act.Fori(1, G - 1) as i:
                for c in range(CH):
                    chunk(i, c, True)
            for c in range(CH):
                chunk(G - 1, c, False, last=c == CH - 1)
            z1_out(CH - 1, NQ, slots_of(G - 1, CH - 1, True)[-1].done)

            act.wait_ge(setup_c, 16 * 15)
            act.wait_ge(z2_sum, 2 * G)
            nc.scalar.activation(z2r[:, :], z2s[:, :, :].rearrange("p g b -> p (g b)"), ACT.Relu,
                                 bias=b2t[:, :]).then_inc(z2_relu, 1)
            act.wait_ge(z2_row, 1)
            for bq in range(4):
                nc.scalar.copy(aux[32:36, bq, :], pV[0:4, :]).then_inc(aux_ready, 1)

            def hid1_out(bq):
                for m in range(4):
                    act.wait_ge(hid1_done, 4 * bq + m + 1)
                    if bq >= 2 and m == 0:
                        act.wait_ge(hid2_done, 2 * (bq - 1))
                    nc.scalar.activation(hid1[:, bq % 2, m, :], pB[:, m // 2, m % 2, :], ACT.Relu,
                                         bias=bt1[:, m:m + 1]).then_inc(hid1_act, 1)

            def hid2_out(bq):
                for m in range(2):
                    act.wait_ge(hid2_done, 2 * bq + m + 1)
                    if bq >= 2 and m == 0:
                        act.wait_ge(y_done, bq - 1)
                    nc.scalar.activation(hid2[:, bq % 2, m, :], pz1[:, m, :], ACT.Relu,
                                         bias=bt2[:, m:m + 1]).then_inc(hid2_act, 1)

            hid1_out(0)
            for bq in range(4):
                if bq < 3:
                    hid1_out(bq + 1)
                hid2_out(bq)
                act.wait_ge(y_done, bq + 1)
                nc.scalar.copy(y[0:1, bq, :], pz0[0:1, :]).then_inc(y_copied, 1)

        @block.tensor
        def _(pe):
            def broadcast(x):
                if x.spread != "pe":
                    return
                if x.bank_free is not None:
                    pe.wait_ge(made_v, x.bank_free)
                if x.kind == "L0" and x.tile == 0:
                    pe.wait_ge(piece_loaded[x.piece], (x.group + 1) * (16 * PIECE_DMAS))
                first, n = {"L0": (2 * x.tile, 2), "L0x": (4, 1), "L1": (5 + 2 * x.tile, 2)}[x.kind]
                for t in range(n):
                    k = SEL_TILES.index(first + t)
                    last = nc.tensor.matmul(pB[:, x.bank, t, :], Sel[:, k, :], S[:, x.piece, :],
                                            start=True, stop=True)
                last.then_inc(bcast_ready, 1)

            def main(x):
                if x.split:
                    pe.wait_ge(lo_ready, x.parts)
                else:
                    pe.wait_ge(made_g, x.made_g)
                if x.kind == "L0x":
                    nc.tensor.matmul(pz0[:, :], Wlo[:, 4, :], Pxparts[:, :], start=False, stop=False)
                    last = nc.tensor.matmul(pz0[:, :], Whi[:, 4, :], Pxparts[:, :], start=False, stop=True)
                    last.then_inc(main_done, 1)
                    return
                if x.kind == "L0":
                    acc, first, opens, closes = pz0[:, :], 2 * x.tile, x.tile == 0, False
                    if opens and not (isinstance(x.q, int) and x.q == 0):
                        pe.wait_ge(z0_read, x.q)
                else:
                    acc, first, opens, closes = pz1[:, x.piece % 2, :], 5 + 2 * x.tile, x.tile == 0, x.tile == 7
                    if opens and not (isinstance(x.q, int) and x.q < 2):
                        pe.wait_ge(z1_read, x.q - 1)
                for t in range(2):
                    if x.split:
                        hi, lo = Phi[:, x.part, t, :], Plo[:, x.part, t, :]
                        nc.tensor.matmul(acc, Wlo[:, first + t, :], hi, start=opens and t == 0, stop=False)
                        nc.tensor.matmul(acc, Whi[:, first + t, :], hi, start=False, stop=False)
                        last = nc.tensor.matmul(acc, Whi[:, first + t, :], lo, start=False, stop=closes and t == 1)
                    else:
                        last = nc.tensor.matmul(acc, Wf[:, WHOLE_TILES.index(first + t), :], Pg[:, x.p, t, :],
                                                start=opens and t == 0, stop=closes and t == 1)
                last.then_inc(main_done, 1)

            def layer2(g, c, q):
                pe.wait_ge(h1lo_ready, q)
                if c % 4 == 0 and not (isinstance(g, int) and g == 0 and c == 0):
                    pe.wait_ge(q_done, 2 * g + c // 4)
                nc.tensor.matmul(pV[:, :], W2p[:, 1, c % 4, :], h1[:, :], start=c % 4 == 0, stop=False)
                nc.tensor.matmul(pV[:, :], W2p[:, 0, c % 4, :], h1[:, :], start=False,
                                 stop=c % 4 == 3).then_inc(v_done, 1)

            def chunk(g, c, last=False):
                q = CH * g + c
                slots = slots_of(g, c, last)
                first = isinstance(g, int) and g == 0 and c == 0
                for s, x in enumerate(slots):
                    broadcast(x)
                    behind = back(g, c, s, LAG, slots)
                    if behind is not None:
                        main(behind)
                    if s == min(AT_V, len(slots) - 1) and not first:
                        layer2(g if c else g - 1, (c - 1) % CH, q)

            pe.wait_ge(setup_w, 16 * 9)
            pe.wait_ge(ws_laid, 1)
            for k in range(L0_TILES):
                last = nc.tensor.transpose(pz0[:, 128 * k:128 * k + 128], ws[:, k, :], ident[:, :])
            last.then_inc(w_turned, 1)
            nc.tensor.transpose(pV[:, 0:128], ws[:, 4, :], ident[:, :]).then_inc(w_turned, 1)
            pe.wait_ge(w1_laid, 1)
            for k in range(L1_TILES):
                last = nc.tensor.transpose(pB[:, k // 8, (k // 4) % 2, 128 * (k % 4):128 * (k % 4) + 128],
                                           w1p[:, 128 * k:128 * k + 128], ident[:, :])
            last.then_inc(w_turned, 1)
            pe.wait_ge(w_lo, 4)
            for g in range(G):
                last = nc.tensor.transpose(pB[0:DENSE, g // 8, (g // 4) % 2, 128 * (g % 4):128 * (g % 4) + 128],
                                           dense[:, g, :], ident[:, :])
            last.then_inc(dense_turned, 1)
            pe.wait_ge(dense_ready, 1)
            pe.wait_ge(sel_ready, 1)
            pe.wait_ge(zeroed, 1)

            for x in prologue_slots():
                broadcast(x)
            for x in prologue_slots():
                main(x)
            for c in range(CH):
                chunk(0, c)
            with pe.Fori(1, G - 1) as i:
                for c in range(CH):
                    chunk(i, c)
            for c in range(CH):
                chunk(G - 1, c, last=c == CH - 1)
            for x in slots_of(G - 1, CH - 1, True)[-LAG:]:
                main(x)

            def features_to_hid1(bq, m):
                if bq >= 1:
                    pe.wait_ge(hid1_act, 4 * (bq - 1) + m + 1)
                nc.tensor.matmul(pB[:, m // 2, m % 2, :], wt1[:, 128 * m:128 * m + 128], feat[:, bq, :],
                                 start=True, stop=False)

            def aux_to_hid1(bq, m):
                if m == 0:
                    pe.wait_ge(aux_ready, bq + 1)
                nc.tensor.matmul(pB[:, m // 2, m % 2, :], wta[:, bq, 128 * m:128 * m + 128], aux[:, bq, :],
                                 start=False, stop=True).then_inc(hid1_done, 1)

            layer2(G - 1, CH - 1, NQ)
            pe.wait_ge(made_v, slots_of(G - 1, CH - 1, True)[-1].made_v)
            pe.wait_ge(setup_c, 16 * 15)
            pe.wait_ge(direct_used, NQ)
            for m in range(4):
                features_to_hid1(0, m)
            pe.wait_ge(z2_relu, 1)
            nc.tensor.matmul(pV[0:4, :], ones4[:, :], z2r[:, :], start=True, stop=True).then_inc(z2_row, 1)

            def to_hid2(bq):
                for m in range(2):
                    if m == 0:
                        pe.wait_ge(hid1_act, 4 * bq + 4)
                    if bq >= 1:
                        pe.wait_ge(hid2_act, 2 * (bq - 1) + m + 1)
                    for k in range(4):
                        last = nc.tensor.matmul(pz1[:, m, :], wt2[:, k, 128 * m:128 * m + 128],
                                                hid1[:, bq % 2, k, :], start=k == 0, stop=k == 3)
                    last.then_inc(hid2_done, 1)

            def to_y(bq):
                pe.wait_ge(hid2_act, 2 * bq + 2)
                if bq >= 1:
                    pe.wait_ge(y_copied, bq)
                for k in range(2):
                    last = nc.tensor.matmul(pz0[0:1, :], wt3[:, k, :], hid2[:, bq % 2, k, :],
                                            start=k == 0, stop=k == 1)
                last.then_inc(y_done, 1)

            for m in range(4):
                aux_to_hid1(0, m)
            for bq in range(4):
                if bq < 3:
                    for m in range(4):
                        features_to_hid1(bq + 1, m)
                        aux_to_hid1(bq + 1, m)
                to_hid2(bq)
                to_y(bq)


_ARRAYS = ["dense_ctx", "ids", "W_top1", "b_top1", "W_top2", "b_top2", "W_top3",
           "L0_rec_W0", "L0_rec_b0", "L0_rec_W1", "L0_rec_b1", "L0_rec_W2", "L0_rec_b2"]


def _constants():
    import numpy as np

    sel = np.zeros((128, N_TILES, 128), np.float32)
    for part in (0, 1):
        for j in range(128):
            i, shift = j // 4, j % 4
            for t in range(L0_TILES):
                sel[2 * ((i + 4 * t + shift) % 32) + part, t, j] = 1
            sel[2 * ((i + 16) % 32) + part, L0_TILES, j] = 1
            for k in range(L1_TILES):
                sel[2 * (2 * k + j // 64) + part, L0_TILES + 1 + k, j] = 1
    ones = np.zeros((128, 4), np.float32)
    for q in range(4):
        ones[32 * q:32 * q + 32, q] = 1
    return {"sel": sel[:, SEL_TILES, :].reshape(128, -1), "ident": np.eye(128, dtype=np.float32), "ones": ones}


def kernel(**inputs):
    import numpy as np
    import concourse.bacc as bacc
    from concourse.bass_utils import run_bass_kernel_spmd

    nc = bacc.Bacc("TRN2", target_bir_lowering=False, num_devices=1)
    arrays = {}

    def dram(name, a):
        arrays[name] = np.ascontiguousarray(a)
        return nc.dram_tensor(name, a.shape, mybir.dt.from_np(a.dtype), kind="ExternalInput").ap()

    tables = [dram(f"tbl_{f}", np.asarray(inputs[f"tbl_{f}"])) for f in range(F)]
    args = [dram("in_" + n, np.asarray(inputs[n])) for n in _ARRAYS]
    consts = [dram("c_" + n, a) for n, a in _constants().items()]
    out = nc.dram_tensor("y_out", (B, 1), F32, kind="ExternalOutput").ap()
    build(nc, tables, *args, *consts, out)
    r = run_bass_kernel_spmd(nc, [arrays], core_ids=[0])
    return r.results[0]["y_out"]
```
